# Optimizing a Trainium2 kernel written in Bass

```python
import numpy as np
import jax
import jax.numpy as jnp

def _softmax(x, axis=-1):
    return jax.nn.softmax(x, axis=axis)

def _gelu(x):
    return jax.nn.gelu(x, approximate=True)

def _silu(x):
    return jax.nn.silu(x)

def _sigmoid(x):
    return jax.nn.sigmoid(x)

def _layernorm(x, axis=-1, eps=1e-05):
    m = jnp.mean(x, axis=axis, keepdims=True)
    v = jnp.var(x, axis=axis, keepdims=True)
    return (x - m) / jnp.sqrt(v + eps)

def _scatter_add(tgt, idx, src, axis=0):
    return tgt.at[idx].add(src)

def _segment_sum(src, seg, n):
    return jax.ops.segment_sum(src, seg, n)
kernel_name = 'mk_gnn_resnorm_d2_gnn_r8_a8ecce'

def setup_inputs(seed: int=0):
    np.random.seed(seed)
    _w = jnp.asarray

    def _rec_inputs():
        import jax
        import jax.numpy as jnp
        _gk = jax.random.key(seed)
        x = -0.000202 + 1 * jax.random.normal(jax.random.fold_in(_gk, 1), (12500, 128), jnp.float32)
        src = jax.random.randint(jax.random.fold_in(_gk, 2), (200000,), 0, 12500, jnp.int32)
        dst = jax.random.randint(jax.random.fold_in(_gk, 3), (200000,), 0, 12500, jnp.int32)
        _o = jnp.argsort(dst, stable=True)
        src = src[_o]
        dst = dst[_o]
        edge_attr_128 = -5.16925e-05 + 1.00005 * jax.random.normal(jax.random.fold_in(_gk, 11), (200000, 128), jnp.float32)
        return (x, src, dst, edge_attr_128)
    x, src, dst, edge_attr_128 = _rec_inputs()

    def _L0_gnn_setup():
        import jax, jax.numpy as jnp
        import numpy as np
        N, E, D = (6250, 100000, 128)
        LN_EPS = 1e-05
        key = jax.random.key(seed)
        ks = jax.random.split(key, 8)
        x = jax.random.normal(ks[0], (N, D), dtype=jnp.float32)
        edge_index = jax.random.randint(ks[1], (2, E), 0, N, dtype=jnp.int64)
        edge_attr = jax.random.normal(ks[2], (E, D), dtype=jnp.float32)
        s_msg = 1.0 / np.sqrt(2 * D)
        s_upd = 1.0 / np.sqrt(2 * D)
        W_msg = jax.random.uniform(ks[3], (2 * D, D), jnp.float32, -s_msg, s_msg)
        b_msg = jax.random.uniform(ks[4], (D,), jnp.float32, -s_msg, s_msg)
        W_upd = jax.random.uniform(ks[5], (2 * D, D), jnp.float32, -s_upd, s_upd)
        b_upd = jax.random.uniform(ks[6], (D,), jnp.float32, -s_upd, s_upd)
        gamma = jnp.ones((D,), jnp.float32)
        beta = jnp.zeros((D,), jnp.float32)
        return {'x': x, 'edge_index': edge_index, 'edge_attr': edge_attr, 'W_msg': W_msg, 'b_msg': b_msg, 'W_upd': W_upd, 'b_upd': b_upd, 'gamma': gamma, 'beta': beta}
    _L0_gnn_all = _L0_gnn_setup()
    _L0_gnn_in = {k: v for k, v in _L0_gnn_all.items() if k in ('W_msg', 'b_msg', 'W_upd', 'b_upd', 'gamma', 'beta')}
    del _L0_gnn_all

    def _L1_gnn_setup():
        import jax, jax.numpy as jnp
        import numpy as np
        LN_EPS = 1e-05

        def layer_norm(x, g, b):
            mu = jnp.mean(x, axis=-1, keepdims=True)
            var = jnp.mean(jnp.square(x - mu), axis=-1, keepdims=True)
            return (x - mu) * jax.lax.rsqrt(var + LN_EPS) * g + b
        key = jax.random.key(seed)
        ks = jax.random.split(key, 8)
        N, E, D = (12500, 125000, 128)
        node_feat = jax.random.normal(ks[0], (N, D), dtype=jnp.float32)
        edge_index = jax.random.randint(ks[1], (2, E), 0, N, dtype=jnp.int64)
        s = 1.0 / np.sqrt(D)
        return {'node_feat': node_feat, 'edge_index': edge_index, 'layer_idx': 0, 'ln1_g': jnp.ones((D,), jnp.float32), 'ln1_b': jnp.zeros((D,), jnp.float32), 'W_conv': jax.random.normal(ks[2], (D, D), jnp.float32) * s, 'b_conv': jnp.zeros((D,), jnp.float32), 'ln2_g': jnp.ones((D,), jnp.float32), 'ln2_b': jnp.zeros((D,), jnp.float32), 'W1': jax.random.normal(ks[3], (D, 4 * D), jnp.float32) * s, 'b1': jnp.zeros((4 * D,), jnp.float32), 'W2': jax.random.normal(ks[4], (4 * D, D), jnp.float32) * (0.5 * s), 'b2': jnp.zeros((D,), jnp.float32)}
    _L1_gnn_all = _L1_gnn_setup()
    _L1_gnn_in = {k: v for k, v in _L1_gnn_all.items() if k in ('ln1_g', 'ln1_b', 'W_conv', 'b_conv', 'ln2_g', 'ln2_b', 'W1', 'b1', 'W2', 'b2')}
    del _L1_gnn_all
    return {'x': x, 'src': src, 'dst': dst, 'edge_attr_128': edge_attr_128, 'L0_gnn_W_msg': _L0_gnn_in['W_msg'], 'L0_gnn_b_msg': _L0_gnn_in['b_msg'], 'L0_gnn_W_upd': _L0_gnn_in['W_upd'], 'L0_gnn_b_upd': _L0_gnn_in['b_upd'], 'L0_gnn_gamma': _L0_gnn_in['gamma'], 'L0_gnn_beta': _L0_gnn_in['beta'], 'L1_gnn_ln1_g': _L1_gnn_in['ln1_g'], 'L1_gnn_ln1_b': _L1_gnn_in['ln1_b'], 'L1_gnn_W_conv': _L1_gnn_in['W_conv'], 'L1_gnn_b_conv': _L1_gnn_in['b_conv'], 'L1_gnn_ln2_g': _L1_gnn_in['ln2_g'], 'L1_gnn_ln2_b': _L1_gnn_in['ln2_b'], 'L1_gnn_W1': _L1_gnn_in['W1'], 'L1_gnn_b1': _L1_gnn_in['b1'], 'L1_gnn_W2': _L1_gnn_in['W2'], 'L1_gnn_b2': _L1_gnn_in['b2']}

def reference(x, src, dst, edge_attr_128, L0_gnn_W_msg, L0_gnn_b_msg, L0_gnn_W_upd, L0_gnn_b_upd, L0_gnn_gamma, L0_gnn_beta, L1_gnn_ln1_g, L1_gnn_ln1_b, L1_gnn_W_conv, L1_gnn_b_conv, L1_gnn_ln2_g, L1_gnn_ln2_b, L1_gnn_W1, L1_gnn_b1, L1_gnn_W2, L1_gnn_b2):
    import jax
    import jax.numpy as jnp

    def _L0_gnn_ref(x, edge_index, edge_attr, W_msg, b_msg, W_upd, b_upd, gamma, beta):
        import jax, jax.numpy as jnp
        import numpy as np
        N, E, D = (6250, 100000, 128)
        LN_EPS = 1e-05
        src, dst = (edge_index[0], edge_index[1])
        n = x.shape[0]
        msg_in = jnp.concatenate([x[src], edge_attr], axis=-1)
        msg = jax.nn.relu(msg_in @ W_msg + b_msg)
        summed = jax.ops.segment_sum(msg, dst, num_segments=n)
        counts = jax.ops.segment_sum(jnp.ones((msg.shape[0],), x.dtype), dst, num_segments=n)
        mean_msg = summed / jnp.maximum(counts, 1.0)[:, None]
        h = jnp.concatenate([x, mean_msg], axis=-1) @ W_upd + b_upd
        mu = jnp.mean(h, axis=-1, keepdims=True)
        var = jnp.mean(jnp.square(h - mu), axis=-1, keepdims=True)
        h = (h - mu) * jax.lax.rsqrt(var + LN_EPS) * gamma + beta
        return jax.nn.relu(h + x)

    def _L1_gnn_ref(node_feat, edge_index, layer_idx, ln1_g, ln1_b, W_conv, b_conv, ln2_g, ln2_b, W1, b1, W2, b2):
        import jax, jax.numpy as jnp
        import numpy as np
        LN_EPS = 1e-05

        def layer_norm(x, g, b):
            mu = jnp.mean(x, axis=-1, keepdims=True)
            var = jnp.mean(jnp.square(x - mu), axis=-1, keepdims=True)
            return (x - mu) * jax.lax.rsqrt(var + LN_EPS) * g + b
        N = node_feat.shape[0]
        h = jax.nn.gelu(layer_norm(node_feat, ln1_g, ln1_b), approximate=False)
        hW = h @ W_conv
        loops = jnp.arange(N, dtype=edge_index.dtype)
        src = jnp.concatenate([edge_index[0], loops])
        dst = jnp.concatenate([edge_index[1], loops])
        deg = jax.ops.segment_sum(jnp.ones(src.shape, hW.dtype), dst, num_segments=N)
        dinv = jnp.where(deg > 0, jax.lax.rsqrt(deg), 0.0)
        coef = dinv[src] * dinv[dst]
        agg = jax.ops.segment_sum(hW[src] * coef[:, None], dst, num_segments=N)
        conv_feat = node_feat + agg + b_conv
        f = layer_norm(conv_feat, ln2_g, ln2_b)
        f = jax.nn.gelu(f @ W1 + b1, approximate=False)
        f = jax.nn.gelu(f @ W2 + b2, approximate=False)
        return node_feat + f
    edge_index = jnp.stack([src, dst])
    x = _layernorm(x + _L0_gnn_ref(x, edge_index, edge_attr_128, L0_gnn_W_msg, L0_gnn_b_msg, L0_gnn_W_upd, L0_gnn_b_upd, L0_gnn_gamma, L0_gnn_beta), axis=-1)
    x = _layernorm(x + _L1_gnn_ref(x, edge_index, 0, L1_gnn_ln1_g, L1_gnn_ln1_b, L1_gnn_W_conv, L1_gnn_b_conv, L1_gnn_ln2_g, L1_gnn_ln2_b, L1_gnn_W1, L1_gnn_b1, L1_gnn_W2, L1_gnn_b2), axis=-1)
    return x

_drawn_inputs = setup_inputs


def setup_inputs(seed=0):
    import zlib

    import numpy as np

    out = dict(_drawn_inputs(seed))
    spreads = {'L0_gnn_gamma': (1.0, 0.2),
     'L0_gnn_beta': (0.0, 0.1),
     'L1_gnn_ln1_g': (1.0, 0.6),
     'L1_gnn_ln1_b': (0.0, 0.8),
     'L1_gnn_b_conv': (0.0, 0.384),
     'L1_gnn_ln2_g': (1.0, 0.2),
     'L1_gnn_ln2_b': (0.0, 0.349),
     'L1_gnn_b1': (0.0, 0.392),
     'L1_gnn_b2': (0.0, 0.1)}
    factors = {'L0_gnn_b_msg': 6.906}
    for name, (base, spread) in spreads.items():
        noise = np.random.default_rng([zlib.crc32(name.encode()), seed]).standard_normal(out[name].shape)
        drawn = base * np.exp(spread * noise) if base else spread * noise
        out[name] = jnp.asarray(drawn.astype(out[name].dtype))
    for name, factor in factors.items():
        out[name] = (out[name] * factor).astype(out[name].dtype)
    return out
```

```python
from contextlib import ExitStack

import concourse.bass as bass
from concourse import mybir

F32 = mybir.dt.float32
BF16 = mybir.dt.bfloat16
I32 = mybir.dt.int32
ALU = mybir.AluOpType
ACT = mybir.ActivationFunctionType
AX = mybir.AxisListType

P = 128
D = 128
N = 12500
E = 200000
J = 4
GROUP = J * P
GROUPS = -(-E // GROUP)
TAIL_E = (E - (GROUPS - 1) * GROUP) // J
BATCHES = -(-N // GROUP)
TAIL_N = (N - (BATCHES - 1) * GROUP) // J
WINDOW = 64
SUMS = N + WINDOW
QUADS = -(-GROUPS // P)
QROWS = [min(P, GROUPS - q * P) for q in range(QUADS)]
HIDDEN = 4 * D
EPS = 1e-5
UE = 6
UN = 6


class Steps:

    def __init__(self, unroll, head=None):
        self.unroll, self.head = unroll, head or unroll

    def item(self, i, k):
        return i * self.unroll + k

    def done(self, i, k, per=1):
        return (i * self.unroll + (k + 1)) * per

    def landed(self, i, k, slots, per=16):
        return (i * (self.unroll // slots) + (k // slots + 1)) * per

    def reuse(self, eng, sem, i, k, slots, per=1):
        if isinstance(i, int) and k < slots:
            return
        assert k >= slots
        eng.wait_ge(sem, (i * self.unroll + (k - slots + 1)) * per)

    def run(self, eng, count, stages):
        lags = [lag for lag, _ in stages]
        whole = (count - 1 + min(min(lags), 0) - self.head) // self.unroll

        def step(i, t):
            for lag, stage in stages:
                if not isinstance(i, int) or 0 <= t - lag < count:
                    stage(i, t - lag)

        for t in range(min(min(lags), 0), self.head):
            step(0, t)
        with eng.Fori(0, whole) as i:
            for s in range(self.unroll):
                step(i, self.head + s)
        for t in range(self.head + self.unroll * whole, count + max(lags)):
            step(0, t)


def after(eng, turn, sem, value):
    eng.wait_ge(sem, value)
    eng.sem_inc(turn, 1)


def bc(ap, shape):
    return ap.broadcast_to(shape)


def build(nc, x, src, dst, edge, Wm, bm, Wu, bu, gamma, beta, g1, b1ln, Wc, bconv, g2, b2ln, W1, b1, W2, b2, out):
    ctx = ExitStack()
    with ctx:
        def sb(name, shape, dt=F32, where=ctx):
            return where.enter_context(nc.sbuf_tensor(name, shape, dt))

        def ps(name, shape, where):
            return where.enter_context(nc.psum_tensor(name, shape, F32))

        table0 = nc.dram_tensor("table0", (N, D), F32).ap()
        table1 = nc.dram_tensor("table1", (N, D), F32).ap()
        x1_dram = nc.dram_tensor("x1_dram", (N, D), F32).ap()
        count_dram = nc.dram_tensor("count_dram", (N,), F32).ap()
        inv_dram = nc.dram_tensor("inv_dram", (N,), F32).ap()

        sums = sb("sums", [P, SUMS])
        row = sb("row", [1, SUMS])
        rel = sb("rel", [P, GROUPS, J])
        srci = sb("srci", [P, GROUPS, J], I32)
        least = sb("least", [P, GROUPS])
        base_f = sb("base_f", [1, GROUPS])
        base_i = sb("base_i", [1, GROUPS], I32)
        win0 = sb("win0", [P, WINDOW])
        win = sb("win", [P, WINDOW])
        passes_i = sb("passes_i", [1, 1], I32)
        ident = sb("ident", [P, P])
        ones_row = sb("ones_row", [1, P])
        ones_bf = sb("ones_bf", [P, 1], BF16)
        wm = sb("wm", [P, 2, D])
        wu = sb("wu", [P, 2, D])
        wc = sb("wc", [P, D])
        inv = sb("inv", [P, BATCHES, J])
        dinv = sb("dinv", [P, BATCHES, J])
        cnt = sb("cnt", [P, BATCHES, J])
        vec = sb("vec", [P, 8])
        bcv = sb("bcv", [P, 5, D])
        brow = sb("brow", [1, 2, D])
        mhalf = sb("mhalf", [P, BATCHES * J])
        BM, GA, BE, BCV = range(4)

        steps_e, steps_n = Steps(UE), Steps(UN)

        class Sems:

            def __init__(self, phase, name):
                self.phase, self.name, self.nums = phase, name, []

            def __call__(self, name):
                s = self.phase.enter_context(nc.semaphore(self.name + name))
                self.nums.append(s.num)
                return s

            def join(self):
                lo, hi = min(self.nums), max(self.nums)
                assert sorted(self.nums) == list(range(lo, hi + 1))
                nc.all_engine_barrier(sems_to_clear=range(lo, hi + 1))

        def rows_of(t, b, part):
            if isinstance(b, int):
                return t[b * GROUP:b * GROUP + part * J, :].rearrange("(p j) d -> p j d", j=J)
            return t[bass.ds(b * GROUP, GROUP), :].rearrange("(p j) d -> p j d", j=J)

        def nodes_of(t, b, part):
            return t[:, bass.ds(b * GROUP, part * J)].rearrange("d (p j) -> d j p", j=J)

        def is_tail(i, k):
            return isinstance(i, int) and k == BATCHES - 1

        with ExitStack() as ph:
            ids = sb("ids", [P, 2, QUADS, GROUP], I32, ph)
            idf = sb("idf", [P, 2, QUADS, GROUP], F32, ph)
            lo = sb("lo", [P, QUADS], F32, ph)
            hi = sb("hi", [P, QUADS], F32, ph)
            lo_bc = sb("lo_bc", [P, QUADS, P], F32, ph)
            spanT = sb("spanT", [QUADS, 2], F32, ph)
            span1 = sb("span1", [1, 2], F32, ph)
            span_i = sb("span_i", [1, 1], I32, ph)
            xb = sb("xb", [P, 2, J, D], F32, ph)
            xT = sb("xT", [P, 2, GROUP], F32, ph)
            tb = sb("tb", [P, 2, J, D], F32, ph)
            vrows = sb("vrows", [8, D], F32, ph)
            win_i = sb("win_i", [P, WINDOW], I32, ph)
            ps_t = ps("ps_t", [P, 2, J, P], ph)
            ps_x = ps("ps_x", [P, 2, J, P], ph)
            ps_m = ps("ps_m", [P, 2, J, D], ph)
            ps_s = ps("ps_s", [P, GROUP], ph)

            sem = Sems(ph, "prep_")
            ids_in = sem("ids_in")
            weights_in = sem("weights_in")
            ident_ok = sem("ident_ok")
            iota_ok = sem("iota_ok")
            const_ok = sem("const_ok")
            idf_ok = sem("idf_ok")
            lohi_ok = sem("lohi_ok")
            lobc_ok = sem("lobc_ok")
            id_t = sem("id_t")
            id_ev = sem("id_ev")
            span_t = sem("span_t")
            span_v = sem("span_v")
            rel_ok = sem("rel_ok")
            x_in = [sem(f"x_in{s}") for s in range(2)]
            x_t = sem("x_t")
            x_c = sem("x_c")
            x_m = sem("x_m")
            x_b = sem("x_b")
            tab_out = [sem(f"tab_out{s}") for s in range(2)]

            flat = [dst, src]
            EVAC = [(w, q) for q in range(QUADS) for w in range(2)]
            st = Steps(2, head=4)

            with nc.Block() as block:
                @block.sync
                def _(sp):
                    for w in range(2):
                        for q in range(QUADS):
                            full = QROWS[q] if q < QUADS - 1 else QROWS[q] - 1
                            sp.dma_start(ids[0:full, w, q, :],
                                         flat[w][q * P * GROUP:(q * P + full) * GROUP]
                                         .rearrange("(g e) -> g e", e=GROUP)).then_inc(ids_in, 16)
                        r = QROWS[-1] - 1
                        short = E - (GROUPS - 1) * GROUP
                        sp.dma_start(ids[r:r + 1, w, QUADS - 1, 0:short],
                                     flat[w][E - short:E].rearrange("(g e) -> g e", g=1)).then_inc(ids_in, 16)
                        sp.dma_start(ids[r:r + 1, w, QUADS - 1, short:GROUP],
                                     flat[w][E - GROUP:E - short].rearrange("(g e) -> g e", g=1)).then_inc(ids_in, 16)

                    def load(i, k):
                        part = TAIL_N if is_tail(i, k) else P
                        st.reuse(sp, x_t, i, k, 2)
                        sp.dma_start(xb[0:part, k % 2], rows_of(x, st.item(i, k), part)).then_inc(x_in[k % 2], 16)

                    def store(i, k):
                        part = TAIL_N if is_tail(i, k) else P
                        sp.wait_ge(x_b, st.done(i, k))
                        sp.dma_start(rows_of(table0, st.item(i, k), part), tb[0:part, k % 2]).then_inc(tab_out[k % 2], 16)

                    st.run(sp, BATCHES, [(-1, load), (1, store)])
                    sp.wait_ge(tab_out[0], 16 * ((BATCHES + 1) // 2))
                    sp.wait_ge(tab_out[1], 16 * (BATCHES // 2))

                @block.gpsimd
                def _(pool):
                    pool.memset(ident[:], 0.0).then_inc(ident_ok, 1)
                    pool.wait_ge(ident_ok, 1)
                    pool.affine_select(out=ident[:], in_=ident[:], compare_op=ALU.not_equal, fill=1.0, base=0,
                                       pattern=[[-1, P]], channel_multiplier=1).then_inc(ident_ok, 1)
                    pool.iota(win_i[:], pattern=[[1, WINDOW]], base=0, channel_multiplier=0).then_inc(iota_ok, 1)
                    pool.wait_ge(rel_ok, 1)
                    tail = rel[:, GROUPS - 1, :]
                    pool.affine_select(out=tail, in_=tail, compare_op=ALU.is_ge, fill=-1.0, base=TAIL_E - 1,
                                       pattern=[[0, J]], channel_multiplier=-1).then_inc(rel_ok, 1)

                @block.scalar
                def _(act):
                    def rows(t):
                        return t.rearrange("(a n) -> a n", a=1)

                    loads = [(wm[:], Wm.rearrange("(t p) n -> p t n", p=P)),
                             (bcv[:, BM, :], rows(bm).broadcast_to([P, D])),
                             (wu[:], Wu.rearrange("(t p) n -> p t n", p=P)), (wc[:], Wc),
                             (bcv[:, GA, :], rows(gamma).broadcast_to([P, D])),
                             (bcv[:, BE, :], rows(beta).broadcast_to([P, D])),
                             (bcv[:, BCV, :], rows(bconv).broadcast_to([P, D])),
                             (vrows[0:1, :], rows(g1)), (vrows[1:2, :], rows(b1ln)),
                             (vrows[2:3, :], rows(g2)), (vrows[3:4, :], rows(b2ln)),
                             (vrows[4:8, :], b1.rearrange("(q n) -> q n", n=D)),
                             (brow[:, 0, :], rows(bu)), (brow[:, 1, :], rows(b2))]
                    for to, what in loads:
                        act.dma_start(to, what).then_inc(weights_in, 16)

                    def copy_x(i, k):
                        part = TAIL_N if is_tail(i, k) else P
                        st.reuse(act, x_m, i, k, 2)
                        act.wait_ge(x_t, st.done(i, k))
                        nc.scalar.copy(xT[:, k % 2, :].rearrange("d (j p) -> d j p", j=J)[:, :, 0:part],
                                       ps_x[:, k % 2, :, 0:part]).then_inc(x_c, 1)

                    st.run(act, BATCHES, [(0, copy_x)])
                    act.wait_ge(weights_in, 16 * len(loads))

                @block.tensor
                def _(pe):
                    pe.wait_ge(ident_ok, 2)
                    for q in range(QUADS):
                        pe.wait_ge(lobc_ok, q + 1)
                        if q >= 1:
                            pe.wait_ge(span_v, q)
                        nc.tensor.transpose(ps_s[:, 0:P], lo_bc[:, q, :], ident[:]).then_inc(span_t, 1)
                    pe.wait_ge(span_v, QUADS)
                    nc.tensor.transpose(ps_s[0:QUADS, 0:P], hi[:], ident[:]).then_inc(span_t, 1)
                    pe.wait_ge(span_v, QUADS + 1)
                    nc.tensor.transpose(ps_s[0:1, 0:QUADS], spanT[:, 0:1], ident[0:QUADS, 0:QUADS]).then_inc(span_t, 1)
                    for n, (w, q) in enumerate(EVAC):
                        if n >= 2:
                            pe.wait_ge(id_ev, n - 1)
                        r = QROWS[q]
                        view = idf[0:r, w, q, :].rearrange("g (p j) -> g j p", j=J)
                        for j in range(J):
                            last = nc.tensor.transpose(ps_t[:, n % 2, j, 0:r], view[:, j, :], ident[0:r, 0:r])
                        last.then_inc(id_t, 1)

                    def transpose_x(i, k):
                        part = TAIL_N if is_tail(i, k) else P
                        pe.wait_ge(x_in[k % 2], st.landed(i, k, 2))
                        st.reuse(pe, x_c, i, k, 2)
                        for j in range(J):
                            last = nc.tensor.transpose(ps_x[:, k % 2, j, 0:part], xb[0:part, k % 2, j, :],
                                                       ident[0:part, 0:part])
                        last.then_inc(x_t, 1)

                    def times_wm(i, k):
                        part = TAIL_N if is_tail(i, k) else P
                        pe.wait_ge(x_c, st.done(i, k))
                        st.reuse(pe, x_b, i, k, 2)
                        for j in range(J):
                            last = nc.tensor.matmul(ps_m[0:part, k % 2, j, :], xT[:, k % 2, j * P:j * P + part],
                                                    wm[:, 0, :], start=True, stop=True)
                        last.then_inc(x_m, 1)

                    pe.wait_ge(weights_in, 16 * 14)
                    pe.wait_ge(span_v, QUADS + 2)
                    nc.tensor.transpose(ps_s[:, 0:8], vrows[:], ident[0:8, 0:8]).then_inc(span_t, 1)
                    st.run(pe, BATCHES, [(0, transpose_x), (1, times_wm)])

                @block.vector
                def _(dve):
                    nc.vector.memset(sums[:], 0.0).then_inc(const_ok, 1)
                    nc.vector.memset(row[:], 0.0).then_inc(const_ok, 1)
                    nc.vector.memset(ones_row[:], 1.0).then_inc(const_ok, 1)
                    nc.vector.memset(ones_bf[:], 1.0).then_inc(const_ok, 1)
                    nc.vector.memset(mhalf[:], -0.5).then_inc(const_ok, 1)
                    nc.vector.memset(cnt[:], 0.0).then_inc(const_ok, 1)
                    nc.vector.memset(lo[:], 0.0).then_inc(const_ok, 1)
                    nc.vector.memset(hi[:], 0.0).then_inc(const_ok, 1)
                    dve.wait_ge(iota_ok, 1)
                    nc.vector.tensor_copy(win0[:], win_i[:]).then_inc(const_ok, 1)
                    dve.wait_ge(const_ok, 9)
                    nc.vector.tensor_copy(win[:], win0[:]).then_inc(const_ok, 1)
                    dve.wait_ge(ids_in, 16 * 2 * (QUADS + 2))
                    n = 0
                    for w in range(2):
                        for q in range(QUADS):
                            n += 1
                            nc.vector.tensor_copy(idf[0:QROWS[q], w, q, :], ids[0:QROWS[q], w, q, :]).then_inc(idf_ok, 1)
                    dve.wait_ge(idf_ok, n)
                    for q in range(QUADS):
                        r = QROWS[q]
                        nc.vector.tensor_reduce(lo[0:r, q:q + 1], idf[0:r, 0, q, :], AX.X, ALU.min).then_inc(lohi_ok, 1)
                        nc.vector.tensor_reduce(hi[0:r, q:q + 1], idf[0:r, 0, q, :], AX.X, ALU.max).then_inc(lohi_ok, 1)
                    dve.wait_ge(lohi_ok, 2 * QUADS)
                    for q in range(QUADS):
                        nc.vector.tensor_copy(lo_bc[:, q, :], bc(lo[:, q:q + 1], [P, P])).then_inc(lobc_ok, 1)
                    dve.wait_ge(lobc_ok, QUADS)
                    nc.vector.tensor_tensor(hi[:], hi[:], lo[:], ALU.subtract).then_inc(lobc_ok, 1)
                    for q in range(QUADS):
                        dve.wait_ge(span_t, q + 1)
                        if q == QUADS - 1:
                            dve.wait_ge(lobc_ok, QUADS + 1)
                        nc.vector.tensor_copy(least[:, q * P:q * P + QROWS[q]], ps_s[:, 0:QROWS[q]]).then_inc(span_v, 1)
                    dve.wait_ge(span_t, QUADS + 1)
                    nc.vector.tensor_reduce(spanT[:, 0:1], ps_s[0:QUADS, 0:P], AX.X, ALU.max).then_inc(span_v, 1)
                    dve.wait_ge(span_t, QUADS + 2)
                    nc.vector.tensor_reduce(span1[:, 0:1], ps_s[0:1, 0:QUADS], AX.X, ALU.max).then_inc(span_v, 1)
                    dve.wait_ge(span_v, QUADS + 2)
                    nc.vector.tensor_scalar(span_i[:], span1[:, 0:1], float(WINDOW), None, ALU.add).then_inc(span_v, 1)
                    dve.wait_ge(span_v, QUADS + 3)
                    nc.vector.tensor_scalar(passes_i[:], span_i[:], WINDOW.bit_length() - 1, None,
                                            ALU.arith_shift_right).then_inc(span_v, 1)
                    nc.vector.tensor_copy(base_f[:], least[0:1, :]).then_inc(span_v, 1)
                    nc.vector.tensor_copy(base_i[:], least[0:1, :]).then_inc(span_v, 1)
                    for n, (w, q) in enumerate(EVAC):
                        dve.wait_ge(id_t, n + 1)
                        to = (rel, srci)[w][:, q * P:q * P + QROWS[q], :].rearrange("p g j -> p j g")
                        nc.vector.tensor_copy(to, ps_t[:, n % 2, :, 0:QROWS[q]]).then_inc(id_ev, 1)
                    dve.wait_ge(id_ev, len(EVAC))
                    nc.vector.tensor_tensor(rel[:], rel[:], bc(least[:].unsqueeze(2), [P, GROUPS, J]),
                                            ALU.subtract).then_inc(rel_ok, 1)
                    dve.wait_ge(weights_in, 16 * 14)
                    dve.wait_ge(span_t, QUADS + 3)
                    nc.vector.tensor_copy(vec[:], ps_s[:, 0:8]).then_inc(const_ok, 1)

                    def add_bm(i, k):
                        part = TAIL_N if is_tail(i, k) else P
                        dve.wait_ge(x_m, st.done(i, k))
                        if not (isinstance(i, int) and k < 2):
                            dve.wait_ge(tab_out[k % 2], st.landed(i, k - 2, 2))
                        nc.vector.tensor_tensor(tb[0:part, k % 2], ps_m[0:part, k % 2],
                                                bc(bcv[0:part, BM:BM + 1, :], [part, J, D]), ALU.add).then_inc(x_b, 1)

                    st.run(dve, BATCHES, [(1, add_bm)])

            sem.join()

        passes = nc.values_load(passes_i[0:1, 0:1], min_val=1, max_val=N // WINDOW + 1)

        def edge_phase(layer, table):
            SL = UE
            L = str(layer)
            with ExitStack() as ph:
                idx = sb("idx" + L, [P, SL, J], I32, ph)
                got = sb("got" + L, [P, SL, J, D], F32, ph)
                hot = sb("hot" + L, [P, 3, J, WINDOW], F32, ph)
                ps_a = [ps(f"ps_a{L}{s}", [P, WINDOW], ph) for s in range(2)]
                sem = Sems(ph, "edges_")
                turn_pool, turn_act = sem("turn_pool"), sem("turn_act")
                got_in = [sem(f"got_in{L}{s}") for s in range(SL)]
                idx_ok = sem("idx_ok" + L)
                hot_ok = sem("hot_ok" + L)
                seg_ok = sem("seg_ok" + L)
                flushed = sem("flushed" + L)
                counted = sem("counted" + L)
                moved = sem("moved" + L)
                if layer == 0:
                    ea = sb("ea", [P, SL, J, D], F32, ph)
                    eaT = sb("eaT", [P, 2, GROUP], F32, ph)
                    msg = sb("msg", [P, 3, J, D], F32, ph)
                    ps_e = [ps(f"ps_e{s}", [P, GROUP], ph) for s in range(2)]
                    ps_p = [ps(f"ps_p{s}", [P, J, D], ph) for s in range(2)]
                    ps_c = [ps(f"ps_c{s}", [1, WINDOW], ph) for s in range(2)]
                    ea_in = [sem(f"ea_in{s}") for s in range(SL)]
                    ea_t = sem("ea_t")
                    ea_c = sem("ea_c")
                    pre_ok = sem("pre_ok")
                    add_ok = sem("add_ok")
                    relu_ok = sem("relu_ok")
                se = steps_e
                got_free = (lambda: add_ok) if layer == 0 else (lambda: seg_ok)
                lag_seg = 2 if layer == 0 else 0

                with nc.Fori(0, passes):
                    with nc.Block() as block:
                        @block.gpsimd
                        def _(pool):
                            def gather(i, k):
                                s = k % SL
                                if not (isinstance(i, int) and k < SL):
                                    after(pool, turn_pool, got_free(), se.done(i, k - SL))
                                after(pool, turn_pool, idx_ok, se.done(i, k))
                                for j in range(J):
                                    pool.indirect_dma_start(
                                        out=got[:, s, j, :], out_offset=None, in_=table,
                                        in_offset=bass.IndirectOffsetOnAxis(ap=idx[:, s, j:j + 1], axis=0)
                                    ).then_inc(got_in[s], 16)

                            se.run(pool, GROUPS, [(0, gather)])

                        @block.sync
                        def _(sp):
                            if layer == 1:
                                return

                            def load(i, k):
                                s = k % SL
                                part = TAIL_E if isinstance(i, int) and k == GROUPS - 1 else P
                                se.reuse(sp, ea_t, i, k, SL)
                                sp.dma_start(ea[0:part, s], rows_of(edge, se.item(i, k), part)).then_inc(ea_in[s], 16)

                            se.run(sp, GROUPS, [(0, load)])

                        @block.scalar
                        def _(act):
                            def indices(i, k):
                                s = k % SL
                                if not (isinstance(i, int) and k < SL):
                                    after(act, turn_act, got_in[s], se.landed(i, k - SL, SL, 16 * J))
                                g = se.item(i, k)
                                src_at = srci[:, g, :] if isinstance(g, int) else \
                                    srci[:, bass.ds(g, 1), :].rearrange("p a j -> p (a j)")
                                nc.scalar.copy(idx[:, s, :], src_at).then_inc(idx_ok, 1)

                            def copy_edges(i, k):
                                se.reuse(act, pre_ok, i, k, 2)
                                act.wait_ge(ea_t, se.done(i, k))
                                nc.scalar.copy(eaT[:, k % 2, :], ps_e[k % 2][:]).then_inc(ea_c, 1)

                            def relu(i, k):
                                act.wait_ge(add_ok, se.done(i, k))
                                nc.scalar.activation(msg[:, k % 3], msg[:, k % 3], ACT.Relu).then_inc(relu_ok, 1)

                            stages = [(-3, indices)]
                            if layer == 0:
                                stages += [(0, copy_edges), (1, relu)]
                            se.run(act, GROUPS, stages)

                        @block.tensor
                        def _(pe):
                            def transpose_edges(i, k):
                                s = k % SL
                                pe.wait_ge(ea_in[s], se.landed(i, k, SL))
                                se.reuse(pe, ea_c, i, k, 2)
                                for j in range(J):
                                    last = nc.tensor.transpose(ps_e[k % 2][:, j * P:(j + 1) * P], ea[:, s, j, :], ident[:])
                                last.then_inc(ea_t, 1)

                            def times_wm(i, k):
                                pe.wait_ge(ea_c, se.done(i, k))
                                se.reuse(pe, add_ok, i, k, 2)
                                for j in range(J):
                                    last = nc.tensor.matmul(ps_p[k % 2][:, j, :], eaT[:, k % 2, j * P:(j + 1) * P],
                                                            wm[:, 1, :], start=True, stop=True)
                                last.then_inc(pre_ok, 1)

                            def segment(i, k):
                                pe.wait_ge(hot_ok, se.done(i, k))
                                if layer == 0:
                                    pe.wait_ge(relu_ok, se.done(i, k))
                                else:
                                    pe.wait_ge(got_in[k % SL], se.landed(i, k, SL, 16 * J))
                                se.reuse(pe, flushed, i, k, 2)
                                for j in range(J):
                                    rows = msg[:, k % 3, j, :] if layer == 0 else got[:, k % SL, j, :]
                                    last = nc.tensor.matmul(ps_a[k % 2][:], rows, hot[:, k % 3, j, :],
                                                            start=(j == 0), stop=(j == J - 1))
                                if layer == 0:
                                    se.reuse(pe, counted, i, k, 2)
                                    ones = hot[:, k % 3].bitcast(BF16).rearrange("p j (w h) -> p j w h", h=2)
                                    for j in range(J):
                                        last = nc.tensor.matmul(ps_c[k % 2][:], ones_bf[:], ones[:, j, :, 1],
                                                                start=(j == 0), stop=(j == J - 1))
                                last.then_inc(seg_ok, 1)

                            if layer == 0:
                                se.run(pe, GROUPS, [(0, transpose_edges), (1, times_wm), (2, segment)])
                            else:
                                se.run(pe, GROUPS, [(0, segment)])

                        @block.vector
                        def _(dve):
                            def one_hot(i, k):
                                se.reuse(dve, seg_ok, i, k, 3)
                                g = se.item(i, k)
                                at = rel[:, bass.ds(g, 1), :].rearrange("p a j -> p (a j)").unsqueeze(2)
                                nc.vector.tensor_tensor(hot[:, k % 3], bc(at, [P, J, WINDOW]),
                                                        bc(win[:].unsqueeze(1), [P, J, WINDOW]),
                                                        ALU.is_equal).then_inc(hot_ok, 1)

                            def add(i, k):
                                s = k % SL
                                dve.wait_ge(got_in[s], se.landed(i, k, SL, 16 * J))
                                dve.wait_ge(pre_ok, se.done(i, k))
                                se.reuse(dve, seg_ok, i, k, 3)
                                nc.vector.tensor_tensor(msg[:, k % 3], ps_p[k % 2][:], got[:, s],
                                                        ALU.add).then_inc(add_ok, 1)

                            def flush(i, k):
                                g = se.item(i, k)
                                first = dve.value_load(base_i[0:1, bass.ds(g, 1)], min_val=0, max_val=N)
                                dve.wait_ge(seg_ok, se.done(i, k))
                                se.reuse(dve, flushed, i, k, 1)
                                to = sums[:, bass.ds(first, WINDOW)]
                                nc.vector.tensor_tensor(to, ps_a[k % 2][:], to, ALU.add).then_inc(flushed, 1)
                                if layer == 0:
                                    se.reuse(dve, counted, i, k, 1)
                                    to = row[:, bass.ds(first, WINDOW)]
                                    nc.vector.tensor_tensor(to, ps_c[k % 2][:], to, ALU.add).then_inc(counted, 1)

                            if layer == 0:
                                se.run(dve, GROUPS, [(0, one_hot), (1, add), (2, flush)])
                            else:
                                se.run(dve, GROUPS, [(-1, one_hot), (1, flush)])
                            dve.wait_ge(seg_ok, GROUPS)
                            nc.vector.tensor_scalar(base_f[:], base_f[:], float(WINDOW), float(N),
                                                    ALU.add, ALU.min).then_inc(moved, 1)
                            nc.vector.tensor_scalar(win[:], win[:], float(WINDOW), None, ALU.add).then_inc(moved, 1)
                            dve.wait_ge(moved, 2)
                            nc.vector.tensor_copy(base_i[:], base_f[:]).then_inc(moved, 1)

                    sem.join()

        edge_phase(0, table0)

        with ExitStack() as ph:
            XS = UN
            xb = sb("c_x", [P, XS, J, D], F32, ph)
            xT = sb("c_xT", [P, 2, J, P], F32, ph)
            aS = sb("c_aS", [P, 2, J, P], F32, ph)
            xbeta = sb("c_xbeta", [P, 2, J, D], F32, ph)
            t1 = sb("c_t1", [P, J, D], F32, ph)
            s0 = sb("c_s0", [P, 2, J, D], F32, ph)
            x1 = sb("c_x1", [P, 3, J, D], F32, ph)
            nrm = sb("c_nrm", [P, J, D], F32, ph)
            hT = sb("c_hT", [P, J, P], F32, ph)
            u = sb("c_u", [P, 2, J, D], F32, ph)
            bn = sb("c_bn", [P, 3, J, 6], F32, ph)
            mv = sb("c_mv", [P, 3, 2, J, 2], F32, ph)
            ne = sb("c_ne", [P, 3, 2, 2, J], F32, ph)
            rs = sb("c_rs", [P, 3, 2, J], F32, ph)
            nb = sb("c_nb", [P, 3, 2, J], F32, ph)
            ps_x = ps("c_psx", [P, J, P], ph)
            ps_i = ps("c_psi", [P, GROUP], ph)
            ps_h = [ps(f"c_psh{s}", [P, J, D], ph) for s in range(2)]
            ps_n = ps("c_psn", [P, J, P], ph)
            ps_u = ps("c_psu", [P, J, D], ph)
            ps_v = ps("c_psv", [P, J, P], ph)

            sem = Sems(ph, "mid_")
            turn_pool, turn_act, turn_dve = sem("turn_pool"), sem("turn_act"), sem("turn_dve")
            x_in = [sem(f"c_xin{s}") for s in range(XS)]
            c = {n: sem("c_" + n) for n in ("cnt", "prep", "prep2", "x_t", "inv_bc", "x_c", "mean", "prod", "xbeta",
                                            "bn", "mv", "ne", "rs", "nb", "t1", "t2", "s0", "x1", "nrm", "n_t",
                                            "gelu", "h_t", "u", "u_t", "init")}
            x1_out = [sem(f"c_x1out{s}") for s in range(3)]
            u_out = [sem(f"c_uout{s}") for s in range(2)]
            bn_ok = [sem(f"c_bnok{n}") for n in range(3)]
            mv_ok = [sem(f"c_mvok{n}") for n in range(3)]
            ne_ok = [sem(f"c_neok{n}") for n in range(3)]
            rs_ok = [sem(f"c_rsok{n}") for n in range(3)]
            nb_ok = [sem(f"c_nbok{n}") for n in range(3)]
            st = steps_n
            WHOLE = BATCHES - 1

            with nc.Block() as block:
                @block.sync
                def _(sp):
                    sp.dma_start(count_dram.rearrange("(a n) -> a n", a=1), row[:, 0:N]).then_inc(c["cnt"], 16)
                    sp.wait_ge(c["cnt"], 16)
                    sp.dma_start(cnt[:, 0:WHOLE, :], count_dram[0:WHOLE * GROUP].rearrange("(b p j) -> p b j", p=P, j=J)
                                 ).then_inc(c["cnt"], 16)
                    sp.dma_start(cnt[0:TAIL_N, WHOLE, :], count_dram[WHOLE * GROUP:N].rearrange("(p j) -> p j", j=J)
                                 ).then_inc(c["cnt"], 16)
                    sp.wait_ge(c["prep"], 3)
                    sp.dma_start(inv_dram[0:WHOLE * GROUP].rearrange("(b p j) -> p b j", p=P, j=J), inv[:, 0:WHOLE, :]
                                 ).then_inc(c["cnt"], 16)
                    sp.dma_start(inv_dram[WHOLE * GROUP:N].rearrange("(p j) -> p j", j=J), inv[0:TAIL_N, WHOLE, :]
                                 ).then_inc(c["cnt"], 16)
                    sp.wait_ge(c["cnt"], 80)
                    sp.dma_start(row[:, 0:N], inv_dram.rearrange("(a n) -> a n", a=1)).then_inc(c["cnt"], 16)

                    def load(i, k):
                        part = TAIL_N if is_tail(i, k) else P
                        st.reuse(sp, c["s0"], i, k, XS)
                        sp.dma_start(xb[0:part, k % XS], rows_of(x, st.item(i, k), part)).then_inc(x_in[k % XS], 16)

                    def store_x1(i, k):
                        part = TAIL_N if is_tail(i, k) else P
                        sp.wait_ge(c["x1"], st.done(i, k))
                        sp.dma_start(rows_of(x1_dram, st.item(i, k), part), x1[0:part, k % 3]).then_inc(x1_out[k % 3], 16)

                    def store_u(i, k):
                        part = TAIL_N if is_tail(i, k) else P
                        sp.wait_ge(c["u"], st.done(i, k))
                        sp.dma_start(rows_of(table1, st.item(i, k), part), u[0:part, k % 2]).then_inc(u_out[k % 2], 16)

                    st.run(sp, BATCHES, [(-1, load), (1, store_x1), (3, store_u)])
                    for s in range(3):
                        sp.wait_ge(x1_out[s], 16 * len(range(s, BATCHES, 3)))
                    for s in range(2):
                        sp.wait_ge(u_out[s], 16 * len(range(s, BATCHES, 2)))

                @block.gpsimd
                def _(pool):
                    pool.wait_ge(c["prep"], 1)
                    pool.tensor_tensor(dinv[:].rearrange("p b j -> p (b j)"), dinv[:].rearrange("p b j -> p (b j)"),
                                       mhalf[:], ALU.pow).then_inc(c["prep2"], 1)

                    def power(n):
                        def stage(i, k):
                            part = TAIL_N if is_tail(i, k) else P
                            s = k % 2
                            after(pool, turn_pool, ne_ok[n], st.done(i, k))
                            if n == 0:
                                st.reuse(pool, c["t2"], i, k, 2)
                            else:
                                st.reuse(pool, c["x1"] if n == 1 else c["nrm"], i, k, 2)
                            pool.tensor_tensor(rs[0:part, n, s, :], ne[0:part, n, s, 1, :], mhalf[0:part, 0:J],
                                               ALU.pow).then_inc(rs_ok[n], 1)
                            if n:
                                pool.wait_ge(rs_ok[n], st.done(i, k))
                                pool.tensor_tensor(nb[0:part, n, s, :], ne[0:part, n, s, 0, :], rs[0:part, n, s, :],
                                                   ALU.mult).then_inc(nb_ok[n], 1)
                        return stage

                    def x_beta(i, k):
                        part = TAIL_N if is_tail(i, k) else P
                        after(pool, turn_pool, x_in[k % XS], st.landed(i, k, XS))
                        st.reuse(pool, c["t2"], i, k, 2)
                        pool.tensor_tensor(xbeta[0:part, k % 2], xb[0:part, k % XS],
                                           bc(bcv[0:part, BE:BE + 1, :], [part, J, D]), ALU.add).then_inc(c["xbeta"], 1)

                    st.run(pool, BATCHES, [(0, x_beta), (2, power(2)), (1, power(1)), (0, power(0))])

                @block.scalar
                def _(act):
                    def copy_x(i, k):
                        part = TAIL_N if is_tail(i, k) else P
                        st.reuse(act, c["prod"], i, k, 2)
                        act.wait_ge(c["x_t"], st.done(i, k))
                        nc.scalar.copy(xT[:, k % 2, :, 0:part], ps_x[:, :, 0:part]).then_inc(c["x_c"], 1)

                    def gelu(i, k):
                        part = TAIL_N if is_tail(i, k) else P
                        st.reuse(act, c["h_t"], i, k, 1)
                        act.wait_ge(c["n_t"], st.done(i, k))
                        nc.scalar.activation(hT[:, :, 0:part], ps_n[:, :, 0:part], ACT.Gelu, bias=vec[:, 1:2],
                                             scale=vec[:, 0:1]).then_inc(c["gelu"], 1)

                    def norm1(i, k):
                        part = TAIL_N if is_tail(i, k) else P
                        act.wait_ge(nb_ok[2], st.done(i, k))
                        st.reuse(act, c["n_t"], i, k, 1)
                        for j in range(J):
                            last = nc.scalar.activation(nrm[0:part, j, :], x1[0:part, k % 3, j, :], ACT.Identity,
                                                        bias=nb[0:part, 2, k % 2, j:j + 1], scale=rs[0:part, 2, k % 2, j:j + 1])
                        last.then_inc(c["nrm"], 1)

                    def norm0(i, k):
                        part = TAIL_N if is_tail(i, k) else P
                        if not (isinstance(i, int) and k < 3):
                            act.wait_ge(x1_out[k % 3], st.landed(i, k - 3, 3))
                            st.reuse(act, c["nrm"], i, k, 3)
                        act.wait_ge(nb_ok[1], st.done(i, k))
                        for j in range(J):
                            last = nc.scalar.activation(x1[0:part, k % 3, j, :], s0[0:part, k % 2, j, :], ACT.Identity,
                                                        bias=nb[0:part, 1, k % 2, j:j + 1], scale=rs[0:part, 1, k % 2, j:j + 1])
                        last.then_inc(c["x1"], 1)

                    def self_loop(i, k):
                        part = TAIL_N if is_tail(i, k) else P
                        after(act, turn_act, c["u_t"], st.done(i, k))
                        nc.scalar.copy(nodes_of(sums, st.item(i, k), part), ps_v[:, :, 0:part]).then_inc(c["init"], 1)

                    st.run(act, BATCHES, [(0, copy_x), (3, gelu), (2, norm1), (1, norm0), (3, self_loop)])

                @block.tensor
                def _(pe):
                    pe.wait_ge(c["cnt"], 96)

                    def transpose_x(i, k):
                        part = TAIL_N if is_tail(i, k) else P
                        pe.wait_ge(x_in[k % XS], st.landed(i, k, XS))
                        st.reuse(pe, c["x_c"], i, k, 1)
                        for j in range(J):
                            last = nc.tensor.transpose(ps_x[:, j, 0:part], xb[0:part, k % XS, j, :], ident[0:part, 0:part])
                        last.then_inc(c["x_t"], 1)
                        st.reuse(pe, c["mean"], i, k, 1)
                        b = st.item(i, k)
                        nc.tensor.matmul(ps_i[:, 0:part * J], ones_row[:], row[:, bass.ds(b * GROUP, part * J)],
                                         start=True, stop=True).then_inc(c["inv_bc"], 1)

                    def update(i, k):
                        part = TAIL_N if is_tail(i, k) else P
                        pe.wait_ge(c["x_c"], st.done(i, k))
                        pe.wait_ge(c["mean"], st.done(i, k))
                        st.reuse(pe, c["t1"], i, k, 2)
                        for j in range(J):
                            to = ps_h[k % 2][0:part, j, :]
                            nc.tensor.matmul(to, xT[:, k % 2, j, 0:part], wu[:, 0, :], start=True, stop=False)
                            nc.tensor.matmul(to, aS[:, k % 2, j, 0:part], wu[:, 1, :], start=False, stop=False)
                            last = nc.tensor.matmul(to, ones_row[:, 0:part], brow[:, 0, :], start=False, stop=True)
                        last.then_inc(c["prod"], 1)

                    def transpose_h(i, k):
                        part = TAIL_N if is_tail(i, k) else P
                        pe.wait_ge(c["gelu"], st.done(i, k))
                        st.reuse(pe, c["u"], i, k, 1)
                        for j in range(J):
                            last = nc.tensor.transpose(ps_u[0:part, j, :], hT[:, j, 0:part], ident[:])
                        last.then_inc(c["h_t"], 1)

                    def transpose_u(i, k):
                        part = TAIL_N if is_tail(i, k) else P
                        pe.wait_ge(c["u"], st.done(i, k))
                        st.reuse(pe, c["init"], i, k, 1)
                        for j in range(J):
                            last = nc.tensor.transpose(ps_v[:, j, 0:part], u[0:part, k % 2, j, :], ident[0:part, 0:part])
                        last.then_inc(c["u_t"], 1)

                    def transpose_n(i, k):
                        part = TAIL_N if is_tail(i, k) else P
                        pe.wait_ge(c["nrm"], st.done(i, k))
                        st.reuse(pe, c["gelu"], i, k, 1)
                        for j in range(J):
                            last = nc.tensor.transpose(ps_n[:, j, 0:part], nrm[0:part, j, :], ident[0:part, 0:part])
                        last.then_inc(c["n_t"], 1)

                    st.run(pe, BATCHES, [(0, transpose_x), (0, update), (3, transpose_h), (3, transpose_u), (2, transpose_n)])

                @block.vector
                def _(dve):
                    nc.vector.tensor_copy(win[:], win0[:]).then_inc(c["prep2"], 1)
                    nc.vector.tensor_copy(base_f[:], least[0:1, :]).then_inc(c["prep2"], 1)
                    nc.vector.tensor_copy(base_i[:], least[0:1, :]).then_inc(c["prep2"], 1)
                    dve.wait_ge(c["cnt"], 48)
                    nc.vector.tensor_scalar(dinv[:], cnt[:], 1.0, None, ALU.add).then_inc(c["prep"], 1)
                    nc.vector.tensor_scalar(inv[:], cnt[:], 1.0, None, ALU.max).then_inc(c["prep"], 1)
                    dve.wait_ge(c["prep"], 2)
                    nc.vector.reciprocal(inv[:], inv[:]).then_inc(c["prep"], 1)
                    dve.wait_ge(c["prep2"], 4)

                    def mean(i, k):
                        part = TAIL_N if is_tail(i, k) else P
                        st.reuse(dve, c["prod"], i, k, 2)
                        dve.wait_ge(c["inv_bc"], st.done(i, k))
                        nc.vector.tensor_tensor(aS[:, k % 2, :, 0:part], nodes_of(sums, st.item(i, k), part),
                                                ps_i[:, 0:part * J].rearrange("d (p j) -> d j p", j=J),
                                                ALU.mult).then_inc(c["mean"], 1)

                    def stats(n, value, ready):
                        def stage(i, k):
                            part = TAIL_N if is_tail(i, k) else P
                            s = k % 2
                            dve.wait_ge(ready, st.done(i, k))
                            st.reuse(dve, mv_ok[n], i, k, 1, J)
                            for j in range(J):
                                last = nc.vector.bn_stats(bn[0:part, n, j, :], value(k, part)[:, j, :])
                            last.then_inc(bn_ok[n], 1)
                            dve.wait_ge(bn_ok[n], st.done(i, k))
                            if n == 0:
                                st.reuse(dve, c["t1"], i, k, 2)
                            st.reuse(dve, ne_ok[n], i, k, 1)
                            dve.sem_inc(turn_dve, 1)
                            for j in range(J):
                                nc.vector.bn_aggr(mv[0:part, n, s, j, :], bn[0:part, n, j, :]).then_inc(mv_ok[n], 1)
                            dve.wait_ge(mv_ok[n], st.done(i, k, J))
                            if n:
                                st.reuse(dve, nb_ok[n], i, k, 2)
                            else:
                                st.reuse(dve, rs_ok[n], i, k, 2)
                            nc.vector.tensor_scalar(ne[0:part, n, s, 0, :], mv[0:part, n, s, :, 0], -1.0, None, ALU.mult)
                            nc.vector.tensor_scalar(ne[0:part, n, s, 1, :], mv[0:part, n, s, :, 1], EPS, None,
                                                    ALU.add).then_inc(ne_ok[n], 1)
                        return stage

                    def layer0_out(i, k):
                        part = TAIL_N if is_tail(i, k) else P
                        s = k % 2
                        dve.wait_ge(mv_ok[0], st.done(i, k, J))
                        st.reuse(dve, c["t2"], i, k, 1)
                        for j in range(J):
                            last = nc.vector.scalar_tensor_tensor(
                                t1[0:part, j, :], ps_h[s][0:part, j, :], mv[0:part, 0, s, j, 0:1],
                                bcv[0:part, GA, :], ALU.subtract, ALU.mult)
                        last.then_inc(c["t1"], 1)
                        dve.wait_ge(c["t1"], st.done(i, k))
                        dve.wait_ge(rs_ok[0], st.done(i, k))
                        dve.wait_ge(c["xbeta"], st.done(i, k))
                        st.reuse(dve, c["x1"], i, k, 2)
                        for j in range(J):
                            last = nc.vector.scalar_tensor_tensor(
                                s0[0:part, s, j, :], t1[0:part, j, :], rs[0:part, 0, s, j:j + 1],
                                xbeta[0:part, s, j, :], ALU.mult, ALU.add)
                        last.then_inc(c["t2"], 1)
                        dve.wait_ge(c["t2"], st.done(i, k))
                        nc.vector.scalar_tensor_tensor(s0[0:part, s], s0[0:part, s], 0.0, xb[0:part, k % XS],
                                                       ALU.max, ALU.add).then_inc(c["s0"], 1)

                    def scale_u(i, k):
                        part = TAIL_N if is_tail(i, k) else P
                        dve.wait_ge(c["h_t"], st.done(i, k))
                        if not (isinstance(i, int) and k < 2):
                            dve.wait_ge(u_out[k % 2], st.landed(i, k - 2, 2))
                            st.reuse(dve, c["u_t"], i, k, 2)
                        b = st.item(i, k)
                        at = dinv[0:part, bass.ds(b, 1), :].rearrange("p a j -> p (a j)").unsqueeze(2)
                        nc.vector.tensor_tensor(u[0:part, k % 2], ps_u[0:part], bc(at, [part, J, D]),
                                                ALU.mult).then_inc(c["u"], 1)

                    st.run(dve, BATCHES, [
                        (0, mean),
                        (2, stats(2, lambda k, part: x1[0:part, k % 3], c["x1"])),
                        (1, layer0_out),
                        (1, stats(1, lambda k, part: s0[0:part, k % 2], c["s0"])),
                        (3, scale_u),
                        (0, stats(0, lambda k, part: ps_h[k % 2][0:part], c["prod"]))])

                    nc.vector.memset(sums[:, N:SUMS], 0.0).then_inc(c["prep2"], 1)

            sem.join()

        edge_phase(1, table1)

        with ExitStack() as ph:
            XS = UN
            x1 = sb("e_x1", [P, XS, J, D], F32, ph)
            xbc = sb("e_xbc", [P, 2, J, D], F32, ph)
            aS = sb("e_aS", [P, 2, J, P], F32, ph)
            z = sb("e_z", [P, 2, J, D], F32, ph)
            nrm = sb("e_nrm", [P, J, D], F32, ph)
            zT = sb("e_zT", [P, 2, J, P], F32, ph)
            w1 = sb("e_w1", [P, HIDDEN], F32, ph)
            w2 = sb("e_w2", [P, J, D], F32, ph)
            fT = sb("e_fT", [P, J, J, P], F32, ph)
            f = sb("e_f", [P, 2, J, D], F32, ph)
            o = sb("e_o", [P, 2, J, D], F32, ph)
            bn = sb("e_bn", [P, 2, J, 6], F32, ph)
            mv = sb("e_mv", [P, 2, 2, J, 2], F32, ph)
            ne = sb("e_ne", [P, 2, 2, 2, J], F32, ph)
            rs = sb("e_rs", [P, 2, 2, J], F32, ph)
            nb = sb("e_nb", [P, 2, 2, J], F32, ph)
            ps_z = ps("e_psz", [P, J, D], ph)
            ps_t = ps("e_pst", [P, J, P], ph)
            ps_f = [ps(f"e_psf{q}", [P, J, P], ph) for q in range(4)]
            ps_o = ps("e_pso", [P, J, D], ph)

            sem = Sems(ph, "last_")
            turn_pool, turn_dve = sem("turn_pool"), sem("turn_dve")
            e = {n: sem("e_" + n) for n in ("w", "aS", "conv", "xbc", "z", "nrm", "n_t", "zT", "up", "gelu", "down",
                                            "f", "s", "o")}
            x_in = [sem(f"e_xin{s}") for s in range(XS)]
            outs = [sem(f"e_out{s}") for s in range(2)]
            bn_e = [sem(f"e_bn{n}") for n in range(2)]
            mv_e = [sem(f"e_mv{n}") for n in range(2)]
            ne_e = [sem(f"e_ne{n}") for n in range(2)]
            rs_e = [sem(f"e_rs{n}") for n in range(2)]
            nb_e = [sem(f"e_nb{n}") for n in range(2)]
            st = steps_n

            with nc.Block() as block:
                @block.sync
                def _(sp):
                    sp.dma_start(w1[:], W1).then_inc(e["w"], 16)
                    sp.dma_start(w2[:], W2.rearrange("(q p) n -> p q n", p=P)).then_inc(e["w"], 16)

                    def load(i, k):
                        part = TAIL_N if is_tail(i, k) else P
                        st.reuse(sp, e["s"], i, k, XS)
                        sp.dma_start(x1[0:part, k % XS], rows_of(x1_dram, st.item(i, k), part)).then_inc(x_in[k % XS], 16)

                    def store(i, k):
                        part = TAIL_N if is_tail(i, k) else P
                        sp.wait_ge(e["o"], st.done(i, k))
                        sp.dma_start(rows_of(out, st.item(i, k), part), o[0:part, k % 2]).then_inc(outs[k % 2], 16)

                    st.run(sp, BATCHES, [(-1, load), (4, store)])
                    for s in range(2):
                        sp.wait_ge(outs[s], 16 * len(range(s, BATCHES, 2)))

                @block.gpsimd
                def _(pool):
                    def x_bconv(i, k):
                        part = TAIL_N if is_tail(i, k) else P
                        after(pool, turn_pool, x_in[k % XS], st.landed(i, k, XS))
                        st.reuse(pool, e["z"], i, k, 2)
                        pool.tensor_tensor(xbc[0:part, k % 2], x1[0:part, k % XS],
                                           bc(bcv[0:part, BCV:BCV + 1, :], [part, J, D]), ALU.add).then_inc(e["xbc"], 1)

                    def power(n):
                        def stage(i, k):
                            part = TAIL_N if is_tail(i, k) else P
                            s = k % 2
                            after(pool, turn_pool, ne_e[n], st.done(i, k))
                            st.reuse(pool, e["nrm"] if n == 0 else e["o"], i, k, 2)
                            pool.tensor_tensor(rs[0:part, n, s, :], ne[0:part, n, s, 1, :], mhalf[0:part, 0:J],
                                               ALU.pow).then_inc(rs_e[n], 1)
                            pool.wait_ge(rs_e[n], st.done(i, k))
                            pool.tensor_tensor(nb[0:part, n, s, :], ne[0:part, n, s, 0, :], rs[0:part, n, s, :],
                                               ALU.mult).then_inc(nb_e[n], 1)
                        return stage

                    st.run(pool, BATCHES, [(0, x_bconv), (0, power(0)), (3, power(1))])

                @block.scalar
                def _(act):
                    def norm2(i, k):
                        part = TAIL_N if is_tail(i, k) else P
                        act.wait_ge(nb_e[0], st.done(i, k))
                        st.reuse(act, e["n_t"], i, k, 1)
                        for j in range(J):
                            last = nc.scalar.activation(nrm[0:part, j, :], z[0:part, k % 2, j, :], ACT.Identity,
                                                        bias=nb[0:part, 0, k % 2, j:j + 1], scale=rs[0:part, 0, k % 2, j:j + 1])
                        last.then_inc(e["nrm"], 1)

                    def affine(i, k):
                        part = TAIL_N if is_tail(i, k) else P
                        act.wait_ge(e["n_t"], st.done(i, k))
                        st.reuse(act, e["up"], i, k, 2, J)
                        nc.scalar.activation(zT[:, k % 2, :, 0:part], ps_t[:, :, 0:part], ACT.Identity, bias=vec[:, 3:4],
                                             scale=vec[:, 2:3]).then_inc(e["zT"], 1)

                    def gelu_up(i, k):
                        part = TAIL_N if is_tail(i, k) else P
                        st.reuse(act, e["down"], i, k, 1)
                        for q in range(4):
                            act.wait_ge(e["up"], st.item(i, k) * J + (q + 1))
                            nc.scalar.activation(fT[:, q, :, 0:part], ps_f[q][:, :, 0:part], ACT.Gelu, bias=vec[:, 4 + q:5 + q]
                                                 ).then_inc(e["gelu"], 1)

                    def gelu_down(i, k):
                        part = TAIL_N if is_tail(i, k) else P
                        act.wait_ge(e["down"], st.done(i, k))
                        st.reuse(act, e["o"], i, k, 2)
                        nc.scalar.activation(f[0:part, k % 2], ps_o[0:part], ACT.Gelu).then_inc(e["f"], 1)

                    def norm3(i, k):
                        part = TAIL_N if is_tail(i, k) else P
                        act.wait_ge(nb_e[1], st.done(i, k))
                        if not (isinstance(i, int) and k < 2):
                            act.wait_ge(outs[k % 2], st.landed(i, k - 2, 2))
                        for j in range(J):
                            last = nc.scalar.activation(o[0:part, k % 2, j, :], f[0:part, k % 2, j, :], ACT.Identity,
                                                        bias=nb[0:part, 1, k % 2, j:j + 1], scale=rs[0:part, 1, k % 2, j:j + 1])
                        last.then_inc(e["o"], 1)

                    st.run(act, BATCHES, [(1, affine), (3, gelu_down), (2, gelu_up), (4, norm3), (0, norm2)])

                @block.tensor
                def _(pe):
                    pe.wait_ge(e["w"], 32)

                    def conv(i, k):
                        part = TAIL_N if is_tail(i, k) else P
                        pe.wait_ge(e["aS"], st.done(i, k))
                        st.reuse(pe, e["z"], i, k, 1)
                        for j in range(J):
                            last = nc.tensor.matmul(ps_z[0:part, j, :], aS[:, k % 2, j, 0:part], wc[:], start=True, stop=True)
                        last.then_inc(e["conv"], 1)

                    def transpose_n(i, k):
                        part = TAIL_N if is_tail(i, k) else P
                        pe.wait_ge(e["nrm"], st.done(i, k))
                        st.reuse(pe, e["zT"], i, k, 1)
                        for j in range(J):
                            last = nc.tensor.transpose(ps_t[:, j, 0:part], nrm[0:part, j, :], ident[0:part, 0:part])
                        last.then_inc(e["n_t"], 1)

                    def up(i, k):
                        part = TAIL_N if is_tail(i, k) else P
                        pe.wait_ge(e["zT"], st.done(i, k))
                        st.reuse(pe, e["gelu"], i, k, 1, J)
                        for q in range(4):
                            nc.tensor.matmul(ps_f[q][:, :, 0:part], w1[:, q * P:(q + 1) * P], zT[:, k % 2, :, 0:part],
                                             start=True, stop=True).then_inc(e["up"], 1)

                    def down(i, k):
                        part = TAIL_N if is_tail(i, k) else P
                        pe.wait_ge(e["gelu"], st.done(i, k, J))
                        st.reuse(pe, e["f"], i, k, 1)
                        for j in range(J):
                            for q in range(4):
                                nc.tensor.matmul(ps_o[0:part, j, :], fT[:, q, j, 0:part], w2[:, q, :],
                                                 start=(q == 0), stop=False)
                            last = nc.tensor.matmul(ps_o[0:part, j, :], ones_row[:, 0:part], brow[:, 1, :],
                                                    start=False, stop=True)
                        last.then_inc(e["down"], 1)

                    st.run(pe, BATCHES, [(0, conv), (1, transpose_n), (3, down), (2, up)])

                @block.vector
                def _(dve):
                    def unweave(i, k):
                        part = TAIL_N if is_tail(i, k) else P
                        st.reuse(dve, e["conv"], i, k, 2)
                        nc.vector.tensor_copy(aS[:, k % 2, :, 0:part], nodes_of(sums, st.item(i, k), part)).then_inc(e["aS"], 1)

                    def stats(n, value, ready):
                        def stage(i, k):
                            part = TAIL_N if is_tail(i, k) else P
                            s = k % 2
                            dve.wait_ge(ready, st.done(i, k))
                            st.reuse(dve, mv_e[n], i, k, 1, J)
                            for j in range(J):
                                last = nc.vector.bn_stats(bn[0:part, n, j, :], value(k, part)[:, j, :])
                            last.then_inc(bn_e[n], 1)
                            dve.wait_ge(bn_e[n], st.done(i, k))
                            st.reuse(dve, ne_e[n], i, k, 1)
                            dve.sem_inc(turn_dve, 1)
                            for j in range(J):
                                nc.vector.bn_aggr(mv[0:part, n, s, j, :], bn[0:part, n, j, :]).then_inc(mv_e[n], 1)
                            dve.wait_ge(mv_e[n], st.done(i, k, J))
                            st.reuse(dve, nb_e[n], i, k, 2)
                            nc.vector.tensor_scalar(ne[0:part, n, s, 0, :], mv[0:part, n, s, :, 0], -1.0, None, ALU.mult)
                            nc.vector.tensor_scalar(ne[0:part, n, s, 1, :], mv[0:part, n, s, :, 1], EPS, None,
                                                    ALU.add).then_inc(ne_e[n], 1)
                        return stage

                    def residual(i, k):
                        part = TAIL_N if is_tail(i, k) else P
                        dve.wait_ge(e["conv"], st.done(i, k))
                        dve.wait_ge(e["xbc"], st.done(i, k))
                        st.reuse(dve, e["nrm"], i, k, 2)
                        b = st.item(i, k)
                        for j in range(J):
                            at = dinv[0:part, bass.ds(b, 1), j]
                            last = nc.vector.scalar_tensor_tensor(z[0:part, k % 2, j, :], ps_z[0:part, j, :], at,
                                                                  xbc[0:part, k % 2, j, :], ALU.mult, ALU.add)
                        last.then_inc(e["z"], 1)

                    def twice(i, k):
                        part = TAIL_N if is_tail(i, k) else P
                        dve.wait_ge(e["f"], st.done(i, k))
                        nc.vector.scalar_tensor_tensor(f[0:part, k % 2], x1[0:part, k % XS], 2.0, f[0:part, k % 2],
                                                       ALU.mult, ALU.add).then_inc(e["s"], 1)

                    st.run(dve, BATCHES, [
                        (-1, unweave), (0, residual), (0, stats(0, lambda k, part: z[0:part, k % 2], e["z"])),
                        (3, twice), (3, stats(1, lambda k, part: f[0:part, k % 2], e["s"]))])


_INS = ["x", "src", "dst", "edge_attr_128", "L0_gnn_W_msg", "L0_gnn_b_msg", "L0_gnn_W_upd", "L0_gnn_b_upd",
        "L0_gnn_gamma", "L0_gnn_beta", "L1_gnn_ln1_g", "L1_gnn_ln1_b", "L1_gnn_W_conv", "L1_gnn_b_conv",
        "L1_gnn_ln2_g", "L1_gnn_ln2_b", "L1_gnn_W1", "L1_gnn_b1", "L1_gnn_W2", "L1_gnn_b2"]


def kernel(**inputs):
    import numpy as np
    import concourse.bacc as bacc
    from concourse.bass_utils import run_bass_kernel_spmd as run

    nc = bacc.Bacc("TRN2", target_bir_lowering=False, num_devices=1)
    arrays, args = {}, []
    for name in _INS:
        a = np.ascontiguousarray(inputs[name])
        arrays[f"in_{name}"] = a
        args.append(nc.dram_tensor(f"in_{name}", a.shape, mybir.dt.from_np(a.dtype), kind="ExternalInput").ap())
    args.append(nc.dram_tensor("out_0", (N, D), F32, kind="ExternalOutput").ap())
    build(nc, *args)
    return run(nc, [arrays], core_ids=[0]).results[0]["out_0"]
```

```python
from contextlib import ExitStack

import concourse.bass as bass
from concourse import mybir

F32 = mybir.dt.float32
BF16 = mybir.dt.bfloat16
I32 = mybir.dt.int32
ALU = mybir.AluOpType
ACT = mybir.ActivationFunctionType
AX = mybir.AxisListType

P = 128
D = 128
N = 12500
E = 200000
J = 4
GROUP = J * P
GROUPS = -(-E // GROUP)
TAIL_E = (E - (GROUPS - 1) * GROUP) // J
BATCHES = -(-N // GROUP)
TAIL_N = (N - (BATCHES - 1) * GROUP) // J
WINDOW = 64
SUMS = N + WINDOW
QUADS = -(-GROUPS // P)
QROWS = [min(P, GROUPS - q * P) for q in range(QUADS)]
HIDDEN = 4 * D
EPS = 1e-5
PACE = round(E / N)
SLACK = 4
SLOTS = 8
AHEAD = 6


def is_loop(i):
    return not isinstance(i, int)


class Steps:

    def __init__(self, unroll, head):
        self.unroll, self.head = unroll, head

    def item(self, i, k):
        return i * self.unroll + k

    def done(self, i, k, per=1):
        return (i * self.unroll + (k + 1)) * per

    def landed(self, i, k, slots, per=16):
        return (i * (self.unroll // slots) + (k // slots + 1)) * per

    def first(self, i, k, slots):
        return not is_loop(i) and k < slots

    def reuse(self, eng, sem, i, k, slots, per=1):
        if not self.first(i, k, slots):
            eng.wait_ge(sem, (i * self.unroll + (k - slots + 1)) * per)

    def run(self, eng, count, stages, between=lambda: None):
        lags = [lag for lag, _ in stages]
        whole = (count - 1 + min(min(lags), 0) - self.head) // self.unroll

        def step(i, t):
            for lag, stage in stages:
                if is_loop(i) or 0 <= t - lag < count:
                    stage(i, t - lag)

        for t in range(min(min(lags), 0), self.head):
            step(0, t)
        between()
        with eng.Fori(0, whole) as i:
            for s in range(self.unroll):
                step(i, self.head + s)
        for t in range(self.head + self.unroll * whole, count + max(lags)):
            step(0, t)


def run_together(eng, edge_stages, node_stages):
    lags = [lag for lag, _ in edge_stages] + [0]
    hops = [hop for hop, _ in node_stages] + [0]
    head = 2 * PACE
    whole = (GROUPS - 1 + min(lags) - head) // PACE
    start = SLACK + 1

    def place(hop):
        return 0 if hop < 0 else start + min(hop * (PACE - start) // HOPS, PACE - 1 - start)

    def step(i, t):
        for lag, stage in edge_stages:
            if is_loop(i) or 0 <= t - lag < GROUPS:
                stage(i, t - lag)
        for hop, stage in node_stages:
            if place(hop) == t % PACE and t // PACE >= 1:
                stage(i, t // PACE - 1)

    for t in range(min(lags), head):
        step(0, t)
    with eng.Fori(0, whole) as i:
        for s in range(PACE):
            step(i, head + s)
    for t in range(head + PACE * whole, PACE * BATCHES):
        step(0, t)
    for _, stage in node_stages:
        stage(0, BATCHES - 1)


HOPS = 18


def after(eng, turn, sem, value):
    eng.wait_ge(sem, value)
    eng.sem_inc(turn, 1)


def spread(ap, shape):
    return ap.broadcast_to(shape)


def build(nc, x, src, dst, edge, Wm, bm, Wu, bu, gamma, beta, g1, b1ln, Wc, bconv, g2, b2ln, W1, b1, W2, b2, out):
    ctx = ExitStack()
    sp, pool, act, pe, dve = nc.sync, nc.gpsimd, nc.scalar, nc.tensor, nc.vector
    with ctx:
        def sb(name, shape, dt=F32, where=ctx):
            return where.enter_context(nc.sbuf_tensor(name, shape, dt))

        def ps(name, shape, where):
            return where.enter_context(nc.psum_tensor(name, shape, F32))

        class Sems:

            def __init__(self, phase, name):
                self.phase, self.name, self.nums = phase, name, []

            def __call__(self, name):
                s = self.phase.enter_context(nc.semaphore(self.name + name))
                self.nums.append(s.num)
                return s

            def join(self):
                nums = sorted(self.nums)
                starts = [n for n in nums if n - 1 not in nums]
                for lo in starts:
                    hi = next(n for n in nums if n >= lo and n + 1 not in nums)
                    nc.all_engine_barrier(sems_to_clear=range(lo, hi + 1))

        table0 = nc.dram_tensor("table0", (N, D), F32).ap()
        table1 = nc.dram_tensor("table1", (N, D), F32).ap()
        x1_dram = nc.dram_tensor("x1_dram", (N, D), F32).ap()

        sums = sb("sums", [P, SUMS])
        row = sb("row", [1, SUMS])
        rel = sb("rel", [P, GROUPS, J])
        srci = sb("srci", [P, GROUPS, J], I32)
        least = sb("least", [P, GROUPS])
        base_f = sb("base_f", [1, GROUPS])
        base_i = sb("base_i", [1, GROUPS], I32)
        win0 = sb("win0", [P, WINDOW])
        win = sb("win", [P, WINDOW])
        choice = sb("choice", [1, 2], I32)
        ident = sb("ident", [P, P])
        ones_row = sb("ones_row", [1, P])
        ones_bf = sb("ones_bf", [P, 1], BF16)
        wm = sb("wm", [P, 2, D])
        wu = sb("wu", [P, 2, D])
        wc = sb("wc", [P, D])
        dinv = sb("dinv", [P, BATCHES, J])
        vec = sb("vec", [P, 8])
        bcv = sb("bcv", [P, 3, D])
        brow = sb("brow", [1, 3, D])
        one_eps = sb("one_eps", [P, 2])
        GA, BE, BCV = range(3)
        BU, B2, BM = range(3)

        def rows_of(t, b, part):
            if isinstance(b, int):
                return t[b * GROUP:b * GROUP + part * J, :].rearrange("(p j) d -> p j d", j=J)
            return t[bass.ds(b * GROUP, GROUP), :].rearrange("(p j) d -> p j d", j=J)

        def nodes_of(t, b, part):
            return t[:, bass.ds(b * GROUP, part * J)].rearrange("d (p j) -> d j p", j=J)

        def part_of(i, k):
            return TAIL_N if not is_loop(i) and k == BATCHES - 1 else P

        with ExitStack() as ph:
            ids = sb("ids", [P, 2, QUADS, GROUP], I32, ph)
            idf = sb("idf", [P, 2, QUADS, GROUP], F32, ph)
            lo = sb("lo", [P, QUADS], F32, ph)
            hi = sb("hi", [P, QUADS], F32, ph)
            lo_bc = sb("lo_bc", [P, QUADS, P], F32, ph)
            spanT = sb("spanT", [QUADS, 1], F32, ph)
            flags = sb("flags", [1, 4], F32, ph)
            span_i = sb("span_i", [1, 1], I32, ph)
            due_i = sb("due_i", [1, PACE * BATCHES], I32, ph)
            due = sb("due", [1, PACE * BATCHES], F32, ph)
            xb = sb("xb", [P, 4, J, D], F32, ph)
            xT = sb("xT", [P, 2, J, P], F32, ph)
            tb = sb("tb", [P, 4, J, D], F32, ph)
            vrows = sb("vrows", [8, D], F32, ph)
            win_i = sb("win_i", [P, WINDOW], I32, ph)
            ps_t = [ps(f"ps_t{s}", [P, J, P], ph) for s in range(2)]
            ps_x = [ps(f"ps_x{s}", [P, J, P], ph) for s in range(2)]
            ps_m = [ps(f"ps_m{s}", [P, J, D], ph) for s in range(2)]
            ps_s = ps("ps_s", [P, GROUP], ph)

            sem = Sems(ph, "prep_")
            ids_in, weights_in, early_in = sem("ids_in"), sem("weights_in"), sem("early_in")
            ident_ok, iota_ok, const_ok, zero_ok = sem("ident_ok"), sem("iota_ok"), sem("const_ok"), sem("zero_ok")
            idf_ok, lohi_ok, lobc_ok, rel_ok = sem("idf_ok"), sem("lohi_ok"), sem("lobc_ok"), sem("rel_ok")
            id_t, id_ev, small_t, small_ev = sem("id_t"), sem("id_ev"), sem("small_t"), sem("small_ev")
            flag_ok = sem("flag_ok")
            x_in = [sem(f"x_in{s}") for s in range(4)]
            x_t, x_c, x_m, x_b = sem("x_t"), sem("x_c"), sem("x_m"), sem("x_b")
            tab_out = [sem(f"tab_out{s}") for s in range(4)]

            flat = [dst, src]
            EVAC = [(w, q) for q in range(QUADS) for w in range(2)]
            st = Steps(4, head=8)

            with nc.Block() as block:
                @block.sync
                def _(_):
                    def load(i, k):
                        part = part_of(i, k)
                        st.reuse(sp, x_t, i, k, 4)
                        sp.dma_start(xb[0:part, k % 4], rows_of(x, st.item(i, k), part)).then_inc(x_in[k % 4], 16)

                    def store(i, k):
                        part = part_of(i, k)
                        sp.wait_ge(x_b, st.done(i, k))
                        sp.dma_start(rows_of(table0, st.item(i, k), part), tb[0:part, k % 4]).then_inc(tab_out[k % 4], 16)

                    st.run(sp, BATCHES, [(-2, load), (1, store)])
                    for s in range(4):
                        sp.wait_ge(tab_out[s], 16 * len(range(s, BATCHES, 4)))

                @block.gpsimd
                def _(_):
                    pool.memset(ident[:], 0.0).then_inc(ident_ok, 1)
                    pool.wait_ge(ident_ok, 1)
                    pool.affine_select(out=ident[:], in_=ident[:], compare_op=ALU.not_equal, fill=1.0, base=0,
                                       pattern=[[-1, P]], channel_multiplier=1).then_inc(ident_ok, 1)
                    pool.iota(win_i[:], pattern=[[1, WINDOW]], base=0, channel_multiplier=0).then_inc(iota_ok, 1)
                    pool.iota(due_i[:], pattern=[[GROUP, BATCHES], [0, PACE]], base=0, channel_multiplier=0
                              ).then_inc(iota_ok, 1)
                    pool.memset(row[:], 0.0).then_inc(zero_ok, 1)
                    pool.memset(sums[:], 0.0).then_inc(zero_ok, 1)
                    pool.wait_ge(rel_ok, 1)
                    tail = rel[:, GROUPS - 1, :]
                    pool.affine_select(out=tail, in_=tail, compare_op=ALU.is_ge, fill=-1.0, base=TAIL_E - 1,
                                       pattern=[[0, J]], channel_multiplier=-1).then_inc(rel_ok, 1)

                def as_row(t):
                    return t.rearrange("(a n) -> a n", a=1)

                late = [(wu[:], Wu.rearrange("(t p) n -> p t n", p=P)), (wc[:], Wc),
                        (bcv[:, GA, :], as_row(gamma).broadcast_to([P, D])),
                        (bcv[:, BE, :], as_row(beta).broadcast_to([P, D])),
                        (bcv[:, BCV, :], as_row(bconv).broadcast_to([P, D])),
                        (vrows[0:1, :], as_row(g1)), (vrows[1:2, :], as_row(b1ln)),
                        (vrows[2:3, :], as_row(g2)), (vrows[3:4, :], as_row(b2ln)),
                        (vrows[4:8, :], b1.rearrange("(q n) -> q n", n=D)),
                        (brow[:, BU, :], as_row(bu)), (brow[:, B2, :], as_row(b2))]

                @block.scalar
                def _(_):
                    short = E - (GROUPS - 1) * GROUP
                    r = QROWS[-1] - 1
                    act.dma_start(wm[:], Wm.rearrange("(t p) n -> p t n", p=P)).then_inc(early_in, 16)
                    act.dma_start(brow[:, BM, :], as_row(bm)).then_inc(early_in, 16)
                    for w in range(2):
                        whole = QUADS - 1
                        act.dma_start(ids[:, w, 0:whole, :], flat[w][0:whole * P * GROUP]
                                      .rearrange("(q g e) -> g q e", g=P, e=GROUP)).then_inc(ids_in, 16)
                        act.dma_start(ids[0:r, w, whole, :], flat[w][whole * P * GROUP:(whole * P + r) * GROUP]
                                      .rearrange("(g e) -> g e", e=GROUP)).then_inc(ids_in, 16)
                        act.dma_start(ids[r:r + 1, w, whole, 0:short], as_row(flat[w][E - short:E])).then_inc(ids_in, 16)
                        act.dma_start(ids[r:r + 1, w, whole, short:GROUP],
                                      as_row(flat[w][E - (GROUP - short):E])).then_inc(ids_in, 16)
                    for to, what in late:
                        act.dma_start(to, what).then_inc(weights_in, 16)

                    def copy_x(i, k):
                        part = part_of(i, k)
                        st.reuse(act, x_m, i, k, 2)
                        act.wait_ge(x_t, st.done(i, k))
                        act.copy(xT[:, k % 2, :, 0:part], ps_x[k % 2][:, :, 0:part]).then_inc(x_c, 1)

                    def copy_t(i, k):
                        part = part_of(i, k)
                        act.wait_ge(x_m, st.done(i, k))
                        if not st.first(i, k, 4):
                            act.wait_ge(tab_out[k % 4], st.landed(i, k - 4, 4))
                        act.copy(tb[0:part, k % 4], ps_m[k % 2][0:part]).then_inc(x_b, 1)

                    st.run(act, BATCHES, [(0, copy_x), (1, copy_t)])

                @block.tensor
                def _(_):
                    pe.wait_ge(ident_ok, 2)
                    pe.wait_ge(const_ok, 3)
                    pe.wait_ge(early_in, 32)

                    def transpose_x(i, k):
                        part = part_of(i, k)
                        pe.wait_ge(x_in[k % 4], st.landed(i, k, 4))
                        st.reuse(pe, x_c, i, k, 2)
                        for j in range(J):
                            last = pe.transpose(ps_x[k % 2][:, j, 0:part], xb[0:part, k % 4, j, :], ident[0:part, 0:part])
                        last.then_inc(x_t, 1)

                    def times_wm(i, k):
                        part = part_of(i, k)
                        pe.wait_ge(x_c, st.done(i, k))
                        st.reuse(pe, x_b, i, k, 2)
                        for j in range(J):
                            to = ps_m[k % 2][0:part, j, :]
                            pe.matmul(to, xT[:, k % 2, j, 0:part], wm[:, 0, :], start=True, stop=False)
                            last = pe.matmul(to, ones_row[:, 0:part], brow[:, BM, :], start=False, stop=True)
                        last.then_inc(x_m, 1)

                    def indices():
                        for q in range(QUADS):
                            pe.wait_ge(lobc_ok, q + 1)
                            if q >= 1:
                                pe.wait_ge(small_ev, q)
                            pe.transpose(ps_s[:, 0:P], lo_bc[:, q, :], ident[:]).then_inc(small_t, 1)
                        for n, (w, q) in enumerate(EVAC):
                            if n >= 2:
                                pe.wait_ge(id_ev, n - 1)
                            r = QROWS[q]
                            view = idf[0:r, w, q, :].rearrange("g (p j) -> g j p", j=J)
                            for j in range(J):
                                last = pe.transpose(ps_t[n % 2][:, j, 0:r], view[:, j, :], ident[0:r, 0:r])
                            last.then_inc(id_t, 1)
                        pe.wait_ge(small_ev, QUADS)
                        pe.transpose(ps_s[0:QUADS, 0:P], hi[:], ident[:]).then_inc(small_t, 1)
                        pe.wait_ge(small_ev, QUADS + 1)
                        pe.transpose(ps_s[0:1, 0:QUADS], spanT[:], ident[0:QUADS, 0:QUADS]).then_inc(small_t, 1)
                        pe.wait_ge(weights_in, 16 * len(late))
                        pe.wait_ge(small_ev, QUADS + 2)
                        pe.transpose(ps_s[:, 0:8], vrows[:], ident[0:8, 0:8]).then_inc(small_t, 1)

                    st.run(pe, BATCHES, [(0, transpose_x), (1, times_wm)], between=indices)

                @block.vector
                def _(_):
                    dve.memset(ones_row[:], 1.0).then_inc(const_ok, 1)
                    dve.memset(ones_bf[:], 1.0).then_inc(const_ok, 1)
                    dve.memset(one_eps[:, 0:1], 1.0).then_inc(const_ok, 1)
                    dve.memset(one_eps[:, 1:2], EPS).then_inc(const_ok, 1)
                    dve.memset(lo[:], 0.0).then_inc(const_ok, 1)
                    dve.memset(hi[:], 0.0).then_inc(const_ok, 1)
                    dve.wait_ge(iota_ok, 2)
                    dve.tensor_copy(win0[:], win_i[:]).then_inc(const_ok, 1)
                    dve.tensor_copy(win[:], win_i[:]).then_inc(const_ok, 1)
                    dve.tensor_copy(due[:], due_i[:]).then_inc(const_ok, 1)
                    dve.wait_ge(const_ok, 9)
                    dve.wait_ge(ids_in, 16 * 8)
                    for w in range(2):
                        dve.tensor_copy(idf[:, w, 0:QUADS - 1, :], ids[:, w, 0:QUADS - 1, :]).then_inc(idf_ok, 1)
                        dve.tensor_copy(idf[0:QROWS[-1], w, QUADS - 1, :], ids[0:QROWS[-1], w, QUADS - 1, :]
                                        ).then_inc(idf_ok, 1)
                        if w == 0:
                            dve.wait_ge(idf_ok, 2)
                            for q0, q1 in ((0, QUADS - 1), (QUADS - 1, QUADS)):
                                r = QROWS[q0]
                                dve.tensor_reduce(lo[0:r, q0:q1], idf[0:r, 0, q0:q1, :], AX.X, ALU.min).then_inc(lohi_ok, 1)
                                dve.tensor_reduce(hi[0:r, q0:q1], idf[0:r, 0, q0:q1, :], AX.X, ALU.max).then_inc(lohi_ok, 1)
                            dve.wait_ge(lohi_ok, 4)
                            for q in range(QUADS):
                                dve.tensor_copy(lo_bc[:, q, :], spread(lo[:, q:q + 1], [P, P])).then_inc(lobc_ok, 1)
                    dve.tensor_tensor(hi[:], hi[:], lo[:], ALU.subtract).then_inc(lobc_ok, 1)
                    dve.wait_ge(idf_ok, 4)
                    dve.wait_ge(lobc_ok, QUADS + 1)
                    for q in range(QUADS):
                        dve.wait_ge(small_t, q + 1)
                        dve.tensor_copy(least[:, q * P:q * P + QROWS[q]], ps_s[:, 0:QROWS[q]]).then_inc(small_ev, 1)
                    for n, (w, q) in enumerate(EVAC):
                        dve.wait_ge(id_t, n + 1)
                        to = (rel, srci)[w][:, q * P:q * P + QROWS[q], :].rearrange("p g j -> p j g")
                        dve.tensor_copy(to, ps_t[n % 2][:, :, 0:QROWS[q]]).then_inc(id_ev, 1)
                    dve.wait_ge(small_t, QUADS + 1)
                    dve.tensor_reduce(spanT[:], ps_s[0:QUADS, 0:P], AX.X, ALU.max).then_inc(small_ev, 1)
                    dve.wait_ge(small_ev, QUADS)
                    dve.wait_ge(id_ev, len(EVAC))
                    dve.tensor_tensor(rel[:], rel[:], spread(least[:].unsqueeze(2), [P, GROUPS, J]),
                                      ALU.subtract).then_inc(rel_ok, 1)
                    dve.tensor_copy(base_f[:], least[0:1, :]).then_inc(flag_ok, 1)
                    dve.tensor_copy(base_i[:], least[0:1, :]).then_inc(flag_ok, 1)
                    late_by = due[:, 0:GROUPS - SLACK]
                    dve.tensor_tensor(late_by, late_by, least[0:1, SLACK:GROUPS], ALU.subtract).then_inc(flag_ok, 1)
                    dve.wait_ge(flag_ok, 3)
                    dve.tensor_reduce(flags[:, 1:2], late_by, AX.X, ALU.max).then_inc(flag_ok, 1)
                    dve.wait_ge(small_t, QUADS + 2)
                    dve.tensor_reduce(flags[:, 0:1], ps_s[0:1, 0:QUADS], AX.X, ALU.max).then_inc(small_ev, 1)
                    dve.wait_ge(small_ev, QUADS + 2)
                    dve.wait_ge(flag_ok, 4)
                    dve.tensor_scalar(span_i[:], flags[:, 0:1], float(WINDOW), None, ALU.add).then_inc(flag_ok, 1)
                    dve.tensor_scalar(flags[:, 2:3], flags[:, 0:1], float(WINDOW), None, ALU.is_lt).then_inc(flag_ok, 1)
                    dve.tensor_scalar(flags[:, 3:4], flags[:, 1:2], 0.0, None, ALU.is_le).then_inc(flag_ok, 1)
                    dve.wait_ge(flag_ok, 7)
                    dve.tensor_scalar(choice[:, 0:1], span_i[:], WINDOW.bit_length() - 1, None,
                                      ALU.arith_shift_right).then_inc(flag_ok, 1)
                    dve.tensor_tensor(choice[:, 1:2], flags[:, 2:3], flags[:, 3:4], ALU.mult).then_inc(flag_ok, 1)
                    dve.wait_ge(small_t, QUADS + 3)
                    dve.tensor_copy(vec[:], ps_s[:, 0:8]).then_inc(small_ev, 1)

            sem.join()

        def edge_stages(layer, ph, sem, se):
            L = sem.name
            table = (table0, table1)[layer]
            idx = sb(L + "idx", [P, SLOTS, J], I32, ph)
            got = sb(L + "got", [P, SLOTS, J, D], F32, ph)
            hot = sb(L + "hot", [P, 4, J, WINDOW], F32, ph)
            banks = [ps(L + f"window{s}", [P, 2 * WINDOW], ph) for s in range(2)]
            win_sum = [bank[:, 0:WINDOW] for bank in banks]
            win_cnt = [bank[0:1, WINDOW:2 * WINDOW] for bank in banks]
            turn_pool, turn_act = sem("turn_pool"), sem("turn_act")
            got_in = [sem(f"got_in{s}") for s in range(SLOTS)]
            idx_ok, hot_ok, seg_ok, flushed = sem("idx_ok"), sem("hot_ok"), sem("seg_ok"), sem("flushed")
            counted = flushed
            if layer == 0:
                counted = sem("counted")
                ea = sb(L + "ea", [P, 4, J, D], F32, ph)
                eaT = sb(L + "eaT", [P, 2, J, P], F32, ph)
                msg = sb(L + "msg", [P, 4, J, D], F32, ph)
                ps_e = ps(L + "ps_e", [P, J, P], ph)
                ps_p = [ps(L + f"ps_p{s}", [P, J, D], ph) for s in range(2)]
                ea_in = [sem(f"ea_in{s}") for s in range(4)]
                ea_t, ea_c, pre_ok, add_ok, relu_ok = (sem(n) for n in ("ea_t", "ea_c", "pre_ok", "add_ok", "relu_ok"))
            got_used = add_ok if layer == 0 else seg_ok

            def gather(i, k):
                s = k % SLOTS
                if not se.first(i, k, SLOTS):
                    after(pool, turn_pool, got_used, se.done(i, k - SLOTS))
                after(pool, turn_pool, idx_ok, se.done(i, k))
                for j in range(J):
                    pool.indirect_dma_start(
                        out=got[:, s, j, :], out_offset=None, in_=table,
                        in_offset=bass.IndirectOffsetOnAxis(ap=idx[:, s, j:j + 1], axis=0)
                    ).then_inc(got_in[s], 16)

            def gathers_end():
                for s in range(SLOTS):
                    pool.wait_ge(got_in[s], 16 * J * len(range(s, GROUPS, SLOTS)))
                nums = [s.num for s in got_in]
                pool.dma_reset(range(min(nums), max(nums) + 1))

            def load_edges(i, k):
                part = TAIL_E if not is_loop(i) and k == GROUPS - 1 else P
                se.reuse(sp, ea_t, i, k, 4)
                sp.dma_start(ea[0:part, k % 4], rows_of(edge, se.item(i, k), part)).then_inc(ea_in[k % 4], 16)

            def lay_indices(i, k):
                s = k % SLOTS
                if not se.first(i, k, SLOTS):
                    after(act, turn_act, got_in[s], se.landed(i, k - SLOTS, SLOTS, 16 * J))
                act.copy(idx[:, s, :], srci[:, bass.ds(se.item(i, k), 1), :].rearrange("p a j -> p (a j)")
                         ).then_inc(idx_ok, 1)

            def copy_edges(i, k):
                se.reuse(act, pre_ok, i, k, 2)
                act.wait_ge(ea_t, se.done(i, k))
                act.copy(eaT[:, k % 2], ps_e[:]).then_inc(ea_c, 1)

            def relu(i, k):
                act.wait_ge(add_ok, se.done(i, k))
                act.activation(msg[:, k % 4], msg[:, k % 4], ACT.Relu).then_inc(relu_ok, 1)

            def transpose_edges(i, k):
                pe.wait_ge(ea_in[k % 4], se.landed(i, k, 4))
                se.reuse(pe, ea_c, i, k, 1)
                for j in range(J):
                    last = pe.transpose(ps_e[:, j, :], ea[:, k % 4, j, :], ident[:])
                last.then_inc(ea_t, 1)

            def times_wm(i, k):
                pe.wait_ge(ea_c, se.done(i, k))
                se.reuse(pe, add_ok, i, k, 2)
                for j in range(J):
                    last = pe.matmul(ps_p[k % 2][:, j, :], eaT[:, k % 2, j, :], wm[:, 1, :], start=True, stop=True)
                last.then_inc(pre_ok, 1)

            def segment(i, k):
                pe.wait_ge(hot_ok, se.done(i, k))
                if layer == 0:
                    pe.wait_ge(relu_ok, se.done(i, k))
                else:
                    pe.wait_ge(got_in[k % SLOTS], se.landed(i, k, SLOTS, 16 * J))
                se.reuse(pe, flushed, i, k, 2)
                if layer == 0:
                    se.reuse(pe, counted, i, k, 2)
                for j in range(J):
                    rows = msg[:, k % 4, j, :] if layer == 0 else got[:, k % SLOTS, j, :]
                    last = pe.matmul(win_sum[k % 2], rows, hot[:, k % 4, j, :], start=(j == 0), stop=(j == J - 1))
                if layer == 0:
                    ones = hot[:, k % 4].bitcast(BF16).rearrange("p j (w h) -> p j w h", h=2)
                    for j in range(J):
                        last = pe.matmul(win_cnt[k % 2], ones_bf[:], ones[:, j, :, 1], start=(j == 0), stop=(j == J - 1))
                last.then_inc(seg_ok, 1)

            def one_hot(i, k):
                se.reuse(dve, seg_ok, i, k, 4)
                at = rel[:, bass.ds(se.item(i, k), 1), :].rearrange("p a j -> p (a j)").unsqueeze(2)
                dve.tensor_tensor(hot[:, k % 4], spread(at, [P, J, WINDOW]), spread(win[:].unsqueeze(1), [P, J, WINDOW]),
                                  ALU.is_equal).then_inc(hot_ok, 1)

            def add(i, k):
                s = k % SLOTS
                dve.wait_ge(got_in[s], se.landed(i, k, SLOTS, 16 * J))
                dve.wait_ge(pre_ok, se.done(i, k))
                se.reuse(dve, seg_ok, i, k, 4)
                dve.tensor_tensor(msg[:, k % 4], ps_p[k % 2][:], got[:, s], ALU.add).then_inc(add_ok, 1)

            def flush(i, k):
                first = dve.value_load(base_i[0:1, bass.ds(se.item(i, k), 1)], min_val=0, max_val=N)
                dve.wait_ge(seg_ok, se.done(i, k))
                se.reuse(dve, flushed, i, k, 1)
                to = sums[:, bass.ds(first, WINDOW)]
                dve.tensor_tensor(to, win_sum[k % 2], to, ALU.add).then_inc(flushed, 1)
                if layer == 0:
                    se.reuse(dve, counted, i, k, 1)
                    to = row[:, bass.ds(first, WINDOW)]
                    dve.tensor_tensor(to, win_cnt[k % 2], to, ALU.add).then_inc(counted, 1)

            if layer == 0:
                stages = {"sp": [(0, load_edges)], "pool": [(0, gather)],
                          "act": [(-AHEAD, lay_indices), (0, copy_edges), (1, relu)],
                          "pe": [(0, transpose_edges), (1, times_wm), (2, segment)],
                          "dve": [(0, one_hot), (1, add), (2, flush)]}
            else:
                stages = {"sp": [], "pool": [(0, gather)], "act": [(-AHEAD, lay_indices)],
                          "pe": [(0, segment)], "dve": [(-1, one_hot), (1, flush)]}
            return stages, gathers_end, flushed, counted, seg_ok

        def normalise(ph, sem, n):
            L = sem.name + f"n{n}_"
            bn = sb(L + "bn", [P, J, 6], F32, ph)
            mv = sb(L + "mv", [P, J, 2], F32, ph)
            sd = sb(L + "sd", [P, J], F32, ph)
            rs = sb(L + "rs", [P, J], F32, ph)
            return bn, mv, sd, rs, [sem(f"{w}{n}") for w in ("bn", "mv", "sd", "rs")]

        def stats(st, turn_dve, norm, value, ready, used, i, k):
            bn, mv, sd, rs, (bn_ok, mv_ok, sd_ok, rs_ok) = norm
            part = part_of(i, k)
            dve.wait_ge(ready, st.done(i, k))
            st.reuse(dve, mv_ok, i, k, 1)
            for j in range(J):
                last = dve.bn_stats(bn[0:part, j, :], value[0:part, j, :])
            last.then_inc(bn_ok, 1)
            st.reuse(dve, used, i, k, 1)
            after(dve, turn_dve, bn_ok, st.done(i, k))
            for j in range(J):
                last = dve.bn_aggr(mv[0:part, j, :], bn[0:part, j, :])
            last.then_inc(mv_ok, 1)

        def root(st, norm, i, k):
            bn, mv, sd, rs, (bn_ok, mv_ok, sd_ok, rs_ok) = norm
            part = part_of(i, k)
            st.reuse(act, rs_ok, i, k, 1, 4)
            act.wait_ge(mv_ok, st.done(i, k))
            act.activation(sd[0:part], mv[0:part, :, 1], ACT.Sqrt, bias=one_eps[0:part, 1:2]).then_inc(sd_ok, 1)

        def inverse(st, norm, used, i, k):
            bn, mv, sd, rs, (bn_ok, mv_ok, sd_ok, rs_ok) = norm
            part = part_of(i, k)
            dve.wait_ge(sd_ok, st.done(i, k))
            st.reuse(dve, used, i, k, 1)
            inverse_root(st, i, k, mv[0:part, :, 1], EPS, sd[0:part], rs[0:part], rs[0:part], rs_ok)

        def inverse_root(st, i, k, value, plus, root_of, y, to, ok):
            def step(n):
                dve.wait_ge(ok, st.item(i, k) * 4 + n)

            dve.reciprocal(y, root_of).then_inc(ok, 1)
            step(1)
            dve.scalar_tensor_tensor(root_of, value, plus, y, ALU.add, ALU.mult).then_inc(ok, 1)
            step(2)
            dve.scalar_tensor_tensor(root_of, root_of, -0.5, y, ALU.mult, ALU.mult).then_inc(ok, 1)
            step(3)
            dve.scalar_tensor_tensor(to, root_of, 1.5, y, ALU.add, ALU.mult).then_inc(ok, 1)
            step(4)

        def scaled(norm, to, value, part):
            bn, mv, sd, rs, _ = norm
            for j in range(J):
                last = dve.tensor_scalar(to[0:part, j, :], value[0:part, j, :], mv[0:part, j, 0:1], rs[0:part, j:j + 1],
                                         ALU.subtract, ALU.mult)
            return last

        def node_stages_0(ph, sem, st, summed):
            L = sem.name
            xb = sb(L + "xb", [P, J, D], F32, ph)
            xT = sb(L + "xT", [P, J, P], F32, ph)
            aS = sb(L + "aS", [P, J, P], F32, ph)
            cr = sb(L + "cr", [1, GROUP], F32, ph)
            dd = sb(L + "dd", [P, 4, J], F32, ph)
            ic = sb(L + "ic", [P, J], F32, ph)
            h = sb(L + "h", [P, J, D], F32, ph)
            x1 = sb(L + "x1", [P, J, D], F32, ph)
            nrm = sb(L + "nrm", [P, J, D], F32, ph)
            hT = sb(L + "hT", [P, J, P], F32, ph)
            u = sb(L + "u", [P, J, D], F32, ph)
            ps_t = ps(L + "ps_t", [P, J, P], ph)
            ps_x = ps(L + "ps_x", [P, J, D], ph)
            ps_a = ps(L + "ps_a", [P, J, D], ph)
            turn_act, turn_dve = sem("node_turn_act"), sem("node_turn_dve")
            c = {n: sem("node_" + n) for n in ("x_in", "cr", "aS", "x_t", "cnt", "x_c", "dd", "mx", "dinv", "ic", "px", "mean",
                                               "h", "t1", "t2", "s", "x1", "x1_out", "nrm", "n_t", "gelu", "h_t", "u",
                                               "u_out", "u_t", "init")}
            norm = [normalise(ph, sem, n) for n in range(3)]

            def load_x(i, k):
                part = part_of(i, k)
                st.reuse(sp, c["s"], i, k, 1)
                sp.dma_start(xb[0:part], rows_of(x, st.item(i, k), part)).then_inc(c["x_in"], 16)

            def copy_counts(i, k):
                part = part_of(i, k)
                summed(act, turn_act, i, k)
                if not st.first(i, k, 1):
                    after(act, turn_act, c["cnt"], st.done(i, k - 1))
                act.copy(cr[:, 0:part * J], row[:, bass.ds(st.item(i, k) * GROUP, part * J)]).then_inc(c["cr"], 1)

            def copy_sums(i, k):
                part = part_of(i, k)
                summed(dve, turn_dve, i, k)
                st.reuse(dve, c["px"], i, k, 1)
                dve.tensor_copy(aS[:, :, 0:part], nodes_of(sums, st.item(i, k), part)).then_inc(c["aS"], 1)

            def transpose_x(i, k):
                part = part_of(i, k)
                pe.wait_ge(c["x_in"], st.done(i, k, 16))
                st.reuse(pe, c["init"], i, k, 1)
                for j in range(J):
                    last = pe.transpose(ps_t[:, j, 0:part], xb[0:part, j, :], ident[0:part, 0:part])
                last.then_inc(c["x_t"], 1)
                pe.wait_ge(c["cr"], st.done(i, k))
                st.reuse(pe, c["mean"], i, k, 1)
                counts = cr[:, 0:part * J].rearrange("a (p j) -> a j p", j=J)
                for j in range(J):
                    last = pe.matmul(ps_a[0:part, 0, j:j + 1], counts[:, j, :], ones_row[:, 0:1], start=True, stop=True)
                last.then_inc(c["cnt"], 1)

            def copy_x(i, k):
                part = part_of(i, k)
                st.reuse(act, c["px"], i, k, 1)
                act.wait_ge(c["x_t"], st.done(i, k))
                act.copy(xT[:, :, 0:part], ps_t[:, :, 0:part]).then_inc(c["x_c"], 1)
                st.reuse(act, c["dinv"], i, k, 1, 4)
                act.wait_ge(c["cnt"], st.done(i, k))
                act.activation(dd[0:part, 0, :], ps_a[0:part, 0, 0:J], ACT.Sqrt, bias=one_eps[0:part, 0:1]).then_inc(c["dd"], 1)

            def inverses(i, k):
                part = part_of(i, k)
                dve.wait_ge(c["dd"], st.done(i, k))
                st.reuse(dve, c["ic"], i, k, 1)
                st.reuse(dve, c["dinv"], i, k, 1, 4)
                dve.tensor_scalar(dd[0:part, 1, :], ps_a[0:part, 0, 0:J], 1.0, None, ALU.max).then_inc(c["mx"], 1)
                dve.tensor_copy(dd[0:part, 2, :], ps_a[0:part, 0, 0:J]).then_inc(c["mx"], 1)
                dve.wait_ge(c["mx"], st.done(i, k, 2))
                to = dinv[0:part, bass.ds(st.item(i, k), 1), :].rearrange("p a j -> p (a j)")
                inverse_root(st, i, k, dd[0:part, 2, :], 1.0, dd[0:part, 0, :], dd[0:part, 3, :], to, c["dinv"])
                st.reuse(dve, c["mean"], i, k, 1)
                dve.reciprocal(ic[0:part], dd[0:part, 1, :]).then_inc(c["ic"], 1)

            def products(i, k):
                part = part_of(i, k)
                pe.wait_ge(c["x_c"], st.done(i, k))
                pe.wait_ge(c["aS"], st.done(i, k))
                pe.wait_ge(c["mx"], st.done(i, k, 2))
                st.reuse(pe, c["h"], i, k, 1)
                for j in range(J):
                    pe.matmul(ps_a[0:part, j, :], aS[:, j, 0:part], wu[:, 1, :], start=True, stop=True)
                    pe.matmul(ps_x[0:part, j, :], xT[:, j, 0:part], wu[:, 0, :], start=True, stop=False)
                    last = pe.matmul(ps_x[0:part, j, :], ones_row[:, 0:part], brow[:, BU, :], start=False, stop=True)
                last.then_inc(c["px"], 1)

            def mean(i, k):
                part = part_of(i, k)
                act.wait_ge(c["px"], st.done(i, k))
                act.wait_ge(c["ic"], st.done(i, k))
                if not st.first(i, k, 1):
                    act.wait_ge(c["x1"], st.done(i, k - 1))
                for j in range(J):
                    last = act.activation(h[0:part, j, :], ps_a[0:part, j, :], ACT.Copy, scale=ic[0:part, j:j + 1])
                last.then_inc(c["mean"], 1)

            def update(i, k):
                part = part_of(i, k)
                dve.wait_ge(c["mean"], st.done(i, k))
                dve.tensor_tensor(h[0:part], ps_x[0:part], h[0:part], ALU.add).then_inc(c["h"], 1)
                stats(st, turn_dve, norm[0], h, c["h"], c["t1"], i, k)

            def layer0_out(i, k):
                part = part_of(i, k)
                bn, mv, sd, rs, (bn_ok, mv_ok, sd_ok, rs_ok) = norm[0]
                inverse(st, norm[0], c["t2"], i, k)
                for j in range(J):
                    last = dve.scalar_tensor_tensor(h[0:part, j, :], h[0:part, j, :], mv[0:part, j, 0:1],
                                                    bcv[0:part, GA, :], ALU.subtract, ALU.mult)
                last.then_inc(c["t1"], 1)
                dve.wait_ge(c["t1"], st.done(i, k))
                for j in range(J):
                    last = dve.scalar_tensor_tensor(h[0:part, j, :], h[0:part, j, :], rs[0:part, j:j + 1],
                                                    bcv[0:part, BE, :], ALU.mult, ALU.add)
                last.then_inc(c["t2"], 1)
                dve.wait_ge(c["t2"], st.done(i, k))
                dve.tensor_tensor(h[0:part], h[0:part], xb[0:part], ALU.add).then_inc(c["hx"], 1)
                dve.wait_ge(c["hx"], st.done(i, k))
                dve.scalar_tensor_tensor(h[0:part], h[0:part], 0.0, xb[0:part], ALU.max, ALU.add).then_inc(c["s"], 1)
                stats(st, turn_dve, norm[1], h, c["s"], c["x1"], i, k)

            c["hx"] = sem("node_hx")

            def first_norm(i, k):
                part = part_of(i, k)
                inverse(st, norm[1], c["x1"], i, k)
                if not st.first(i, k, 1):
                    dve.wait_ge(c["x1_out"], st.done(i, k - 1, 16))
                    dve.wait_ge(c["nrm"], st.done(i, k - 1))
                scaled(norm[1], x1, h, part).then_inc(c["x1"], 1)
                stats(st, turn_dve, norm[2], x1, c["x1"], c["nrm"], i, k)

            def second_norm(i, k):
                part = part_of(i, k)
                inverse(st, norm[2], c["nrm"], i, k)
                st.reuse(dve, c["n_t"], i, k, 1)
                scaled(norm[2], nrm, x1, part).then_inc(c["nrm"], 1)

            def store_x1(i, k):
                part = part_of(i, k)
                sp.wait_ge(c["x1"], st.done(i, k))
                sp.dma_start(rows_of(x1_dram, st.item(i, k), part), x1[0:part]).then_inc(c["x1_out"], 16)

            def transpose_n(i, k):
                part = part_of(i, k)
                pe.wait_ge(c["nrm"], st.done(i, k))
                pe.wait_ge(c["x_c"], st.done(i, k))
                for j in range(J):
                    last = pe.transpose(ps_t[:, j, 0:part], nrm[0:part, j, :], ident[0:part, 0:part])
                last.then_inc(c["n_t"], 1)

            def gelu(i, k):
                part = part_of(i, k)
                st.reuse(act, c["h_t"], i, k, 1)
                act.wait_ge(c["n_t"], st.done(i, k))
                act.activation(hT[:, :, 0:part], ps_t[:, :, 0:part], ACT.Gelu, bias=vec[:, 1:2], scale=vec[:, 0:1]
                               ).then_inc(c["gelu"], 1)

            def transpose_h(i, k):
                part = part_of(i, k)
                pe.wait_ge(c["gelu"], st.done(i, k))
                for j in range(J):
                    last = pe.transpose(ps_t[0:part, j, :], hT[:, j, 0:part], ident[:])
                last.then_inc(c["h_t"], 1)

            def scale_u(i, k):
                part = part_of(i, k)
                dve.wait_ge(c["h_t"], st.done(i, k))
                dve.wait_ge(c["dinv"], st.done(i, k, 4))
                if not st.first(i, k, 1):
                    dve.wait_ge(c["u_out"], st.done(i, k - 1, 16))
                    dve.wait_ge(c["u_t"], st.done(i, k - 1))
                at = dinv[0:part, bass.ds(st.item(i, k), 1), :].rearrange("p a j -> p (a j)").unsqueeze(2)
                dve.tensor_tensor(u[0:part], ps_t[0:part], spread(at, [part, J, D]), ALU.mult).then_inc(c["u"], 1)

            def store_u(i, k):
                part = part_of(i, k)
                sp.wait_ge(c["u"], st.done(i, k))
                sp.dma_start(rows_of(table1, st.item(i, k), part), u[0:part]).then_inc(c["u_out"], 16)

            def transpose_u(i, k):
                part = part_of(i, k)
                pe.wait_ge(c["u"], st.done(i, k))
                for j in range(J):
                    last = pe.transpose(ps_t[:, j, 0:part], u[0:part, j, :], ident[0:part, 0:part])
                last.then_inc(c["u_t"], 1)

            def self_loop(i, k):
                part = part_of(i, k)
                after(act, turn_act, c["u_t"], st.done(i, k))
                act.copy(nodes_of(sums, st.item(i, k), part), ps_t[:, :, 0:part]).then_inc(c["init"], 1)

            def ended():
                sp.wait_ge(c["x1_out"], 16 * BATCHES)
                sp.wait_ge(c["u_out"], 16 * BATCHES)

            return {"sp": [(-1, load_x), (11, store_x1), (16, store_u)],
                    "pool": [],
                    "act": [(0, copy_counts), (2, copy_x), (4, mean), (6, lambda i, k: root(st, norm[0], i, k)),
                            (8, lambda i, k: root(st, norm[1], i, k)), (10, lambda i, k: root(st, norm[2], i, k)),
                            (13, gelu), (17, self_loop)],
                    "pe": [(1, transpose_x), (3, products), (12, transpose_n), (14, transpose_h), (16, transpose_u)],
                    "dve": [(0, copy_sums), (3, inverses), (5, update), (7, layer0_out), (9, first_norm),
                            (11, second_norm), (15, scale_u)]}, ended

        def node_stages_1(ph, sem, st, summed):
            L = sem.name
            x1 = sb(L + "x1", [P, J, D], F32, ph)
            z = sb(L + "z", [P, J, D], F32, ph)
            aS = sb(L + "aS", [P, J, P], F32, ph)
            nrm = sb(L + "nrm", [P, J, D], F32, ph)
            zT = sb(L + "zT", [P, J, P], F32, ph)
            w1 = sb(L + "w1", [P, HIDDEN], F32, ph)
            w2 = sb(L + "w2", [P, J, D], F32, ph)
            fT = sb(L + "fT", [P, J, J, P], F32, ph)
            f = sb(L + "f", [P, J, D], F32, ph)
            o = sb(L + "o", [P, J, D], F32, ph)
            ps_z = ps(L + "ps_z", [P, J, D], ph)
            ps_t = ps(L + "ps_t", [P, J, P], ph)
            ps_f = [ps(L + f"ps_f{q}", [P, J, P], ph) for q in range(4)]
            ps_o = ps_z
            turn_dve = sem("node_turn_dve")
            e = {n: sem("node_" + n) for n in ("w", "x_in", "aS", "conv", "xb", "z", "nrm", "n_t", "zT", "up", "gelu",
                                               "down", "f", "s", "o", "out")}
            norm = [normalise(ph, sem, n) for n in range(2)]

            def weights():
                sp.dma_start(w1[:], W1).then_inc(e["w"], 16)
                sp.dma_start(w2[:], W2.rearrange("(q p) n -> p q n", p=P)).then_inc(e["w"], 16)

            def load_x1(i, k):
                part = part_of(i, k)
                st.reuse(sp, e["s"], i, k, 1)
                sp.dma_start(x1[0:part], rows_of(x1_dram, st.item(i, k), part)).then_inc(e["x_in"], 16)

            def copy_sums(i, k):
                part = part_of(i, k)
                summed(dve, turn_dve, i, k)
                st.reuse(dve, e["conv"], i, k, 1)
                dve.tensor_copy(aS[:, :, 0:part], nodes_of(sums, st.item(i, k), part)).then_inc(e["aS"], 1)
                dve.wait_ge(e["x_in"], st.done(i, k, 16))
                st.reuse(dve, e["nrm"], i, k, 1)
                dve.tensor_tensor(z[0:part], x1[0:part], spread(bcv[0:part, BCV:BCV + 1, :], [part, J, D]),
                                  ALU.add).then_inc(e["xb"], 1)

            def conv(i, k):
                part = part_of(i, k)
                pe.wait_ge(e["aS"], st.done(i, k))
                st.reuse(pe, e["f"], i, k, 1)
                for j in range(J):
                    last = pe.matmul(ps_z[0:part, j, :], aS[:, j, 0:part], wc[:], start=True, stop=True)
                last.then_inc(e["conv"], 1)

            def residual(i, k):
                part = part_of(i, k)
                dve.wait_ge(e["conv"], st.done(i, k))
                dve.wait_ge(e["xb"], st.done(i, k))
                for j in range(J):
                    at = dinv[0:part, bass.ds(st.item(i, k), 1), j]
                    last = dve.scalar_tensor_tensor(z[0:part, j, :], ps_z[0:part, j, :], at, z[0:part, j, :],
                                                    ALU.mult, ALU.add)
                last.then_inc(e["z"], 1)
                stats(st, turn_dve, norm[0], z, e["z"], e["nrm"], i, k)

            def norm2(i, k):
                part = part_of(i, k)
                inverse(st, norm[0], e["nrm"], i, k)
                st.reuse(dve, e["n_t"], i, k, 1)
                scaled(norm[0], nrm, z, part).then_inc(e["nrm"], 1)

            def transpose_n(i, k):
                part = part_of(i, k)
                pe.wait_ge(e["nrm"], st.done(i, k))
                st.reuse(pe, e["zT"], i, k, 1)
                for j in range(J):
                    last = pe.transpose(ps_t[:, j, 0:part], nrm[0:part, j, :], ident[0:part, 0:part])
                last.then_inc(e["n_t"], 1)

            def affine(i, k):
                part = part_of(i, k)
                act.wait_ge(e["n_t"], st.done(i, k))
                st.reuse(act, e["up"], i, k, 1, J)
                act.activation(zT[:, :, 0:part], ps_t[:, :, 0:part], ACT.Identity, bias=vec[:, 3:4], scale=vec[:, 2:3]
                               ).then_inc(e["zT"], 1)

            def up(i, k):
                part = part_of(i, k)
                pe.wait_ge(e["zT"], st.done(i, k))
                st.reuse(pe, e["gelu"], i, k, 1, J)
                for q in range(4):
                    pe.matmul(ps_f[q][:, :, 0:part], w1[:, q * P:(q + 1) * P], zT[:, :, 0:part],
                              start=True, stop=True).then_inc(e["up"], 1)

            def gelu_up(i, k):
                part = part_of(i, k)
                st.reuse(act, e["down"], i, k, 1)
                for q in range(4):
                    act.wait_ge(e["up"], st.item(i, k) * J + (q + 1))
                    act.activation(fT[:, q, :, 0:part], ps_f[q][:, :, 0:part], ACT.Gelu, bias=vec[:, 4 + q:5 + q]
                                   ).then_inc(e["gelu"], 1)

            def down(i, k):
                part = part_of(i, k)
                pe.wait_ge(e["gelu"], st.done(i, k, J))
                pe.wait_ge(e["z"], st.done(i, k))
                for j in range(J):
                    for q in range(4):
                        pe.matmul(ps_o[0:part, j, :], fT[:, q, j, 0:part], w2[:, q, :], start=(q == 0), stop=False)
                    last = pe.matmul(ps_o[0:part, j, :], ones_row[:, 0:part], brow[:, B2, :], start=False, stop=True)
                last.then_inc(e["down"], 1)

            def gelu_down(i, k):
                part = part_of(i, k)
                act.wait_ge(e["down"], st.done(i, k))
                st.reuse(act, e["o"], i, k, 1)
                act.activation(f[0:part], ps_o[0:part], ACT.Gelu).then_inc(e["f"], 1)

            def twice(i, k):
                part = part_of(i, k)
                dve.wait_ge(e["f"], st.done(i, k))
                dve.scalar_tensor_tensor(f[0:part], x1[0:part], 2.0, f[0:part], ALU.mult, ALU.add).then_inc(e["s"], 1)
                stats(st, turn_dve, norm[1], f, e["s"], e["o"], i, k)

            def norm3(i, k):
                part = part_of(i, k)
                inverse(st, norm[1], e["o"], i, k)
                if not st.first(i, k, 1):
                    dve.wait_ge(e["out"], st.done(i, k - 1, 16))
                scaled(norm[1], o, f, part).then_inc(e["o"], 1)

            def store(i, k):
                part = part_of(i, k)
                sp.wait_ge(e["o"], st.done(i, k))
                sp.dma_start(rows_of(out, st.item(i, k), part), o[0:part]).then_inc(e["out"], 16)

            def ended():
                sp.wait_ge(e["out"], 16 * BATCHES)

            def weights_ready():
                pe.wait_ge(e["w"], 32)

            return {"sp": [(-1, load_x1), (17, store)],
                    "pool": [],
                    "act": [(3, lambda i, k: root(st, norm[0], i, k)), (6, affine), (8, gelu_up), (11, gelu_down),
                            (14, lambda i, k: root(st, norm[1], i, k))],
                    "pe": [(1, conv), (5, transpose_n), (7, up), (10, down)],
                    "dve": [(0, copy_sums), (2, residual), (4, norm2), (12, twice), (15, norm3)]}, \
                ended, weights, weights_ready

        def windows_reset(done):
            dve.tensor_copy(win[:], win0[:]).then_inc(done, 1)
            dve.tensor_copy(base_f[:], least[0:1, :]).then_inc(done, 1)
            dve.tensor_copy(base_i[:], least[0:1, :]).then_inc(done, 1)

        def node_part(layer, ph, sem, st, summed):
            if layer == 0:
                return node_stages_0(ph, sem, st, summed) + (lambda: None, lambda: None)
            return node_stages_1(ph, sem, st, summed)

        def together(layer):
            with ExitStack() as ph:
                sem = Sems(ph, f"both{layer}_")
                se, st = Steps(PACE, 2 * PACE), Steps(1, 2)
                stages, gathers_end, flushed, counted, seg_ok = edge_stages(layer, ph, sem, se)

                def summed(eng, turn, i, k):
                    groups = GROUPS if not is_loop(i) and k == BATCHES - 1 else (i + (k + 1)) * PACE + SLACK
                    after(eng, turn, flushed if eng is dve else counted, groups)

                nodes, ended, weights, weights_ready = node_part(layer, ph, sem, st, summed)
                with nc.Block() as block:
                    @block.sync
                    def _(_):
                        weights()
                        run_together(sp, stages["sp"], nodes["sp"])
                        ended()

                    @block.gpsimd
                    def _(_):
                        se.run(pool, GROUPS, stages["pool"])
                        gathers_end()

                    @block.scalar
                    def _(_):
                        run_together(act, stages["act"], nodes["act"])

                    @block.tensor
                    def _(_):
                        weights_ready()
                        run_together(pe, stages["pe"], nodes["pe"])

                    @block.vector
                    def _(_):
                        run_together(dve, stages["dve"], nodes["dve"])

                sem.join()

        def apart(layer):
            with ExitStack() as ph:
                sem = Sems(ph, f"edges{layer}_")
                se = Steps(SLOTS, SLOTS)
                stages, gathers_end, flushed, counted, seg_ok = edge_stages(layer, ph, sem, se)
                moved = sem("moved")
                with nc.Fori(0, passes):
                    with nc.Block() as block:
                        @block.sync
                        def _(_):
                            if stages["sp"]:
                                se.run(sp, GROUPS, stages["sp"])

                        @block.gpsimd
                        def _(_):
                            se.run(pool, GROUPS, stages["pool"])
                            gathers_end()

                        @block.scalar
                        def _(_):
                            se.run(act, GROUPS, stages["act"])

                        @block.tensor
                        def _(_):
                            se.run(pe, GROUPS, stages["pe"])

                        @block.vector
                        def _(_):
                            se.run(dve, GROUPS, stages["dve"])
                            dve.wait_ge(seg_ok, GROUPS)
                            dve.tensor_scalar(base_f[:], base_f[:], float(WINDOW), float(N), ALU.add, ALU.min
                                              ).then_inc(moved, 1)
                            dve.tensor_scalar(win[:], win[:], float(WINDOW), None, ALU.add).then_inc(moved, 1)
                            dve.wait_ge(moved, 2)
                            dve.tensor_copy(base_i[:], base_f[:]).then_inc(moved, 1)

                    sem.join()

            with ExitStack() as ph:
                sem = Sems(ph, f"nodes{layer}_")
                st = Steps(1, 2)
                nodes, ended, weights, weights_ready = node_part(layer, ph, sem, st, lambda eng, turn, i, k: None)
                reset = sem("reset")

                def in_turn(eng, stages):
                    st.run(eng, BATCHES, [(0, stage) for _, stage in stages])

                with nc.Block() as block:
                    @block.sync
                    def _(_):
                        weights()
                        in_turn(sp, nodes["sp"])
                        ended()

                    @block.scalar
                    def _(_):
                        in_turn(act, nodes["act"])

                    @block.tensor
                    def _(_):
                        weights_ready()
                        in_turn(pe, nodes["pe"])

                    @block.vector
                    def _(_):
                        windows_reset(reset)
                        in_turn(dve, nodes["dve"])

                sem.join()

        passes = nc.values_load(choice[0:1, 0:1], min_val=1, max_val=N // WINDOW + 1)
        regular = nc.values_load(choice[0:1, 1:2], min_val=0, max_val=1)
        with nc.If(regular == 1):
            together(0)
            together(1)
        with nc.Else():
            apart(0)
            apart(1)


_INS = ["x", "src", "dst", "edge_attr_128", "L0_gnn_W_msg", "L0_gnn_b_msg", "L0_gnn_W_upd", "L0_gnn_b_upd",
        "L0_gnn_gamma", "L0_gnn_beta", "L1_gnn_ln1_g", "L1_gnn_ln1_b", "L1_gnn_W_conv", "L1_gnn_b_conv",
        "L1_gnn_ln2_g", "L1_gnn_ln2_b", "L1_gnn_W1", "L1_gnn_b1", "L1_gnn_W2", "L1_gnn_b2"]


def kernel(**inputs):
    import numpy as np
    import concourse.bacc as bacc
    from concourse.bass_utils import run_bass_kernel_spmd as run

    nc = bacc.Bacc("TRN2", target_bir_lowering=False, num_devices=1)
    arrays, args = {}, []
    for name in _INS:
        a = np.ascontiguousarray(inputs[name])
        arrays[f"in_{name}"] = a
        args.append(nc.dram_tensor(f"in_{name}", a.shape, mybir.dt.from_np(a.dtype), kind="ExternalInput").ap())
    args.append(nc.dram_tensor("out_0", (N, D), F32, kind="ExternalOutput").ap())
    build(nc, *args)
    return run(nc, [arrays], core_ids=[0]).results[0]["out_0"]
```

```python
from contextlib import ExitStack

import concourse.bass as bass
from concourse import mybir

F32 = mybir.dt.float32
BF16 = mybir.dt.bfloat16
I32 = mybir.dt.int32
ALU = mybir.AluOpType
ACT = mybir.ActivationFunctionType
AX = mybir.AxisListType

P = 128
D = 128
N = 12500
E = 200000
J = 4
GROUP = J * P
GROUPS = -(-E // GROUP)
TAIL_E = (E - (GROUPS - 1) * GROUP) // J
BATCHES = -(-N // GROUP)
FIRST_N = (N - (BATCHES - 1) * GROUP) // J
WINDOW = 64
SUMS = N + WINDOW
QUADS = -(-GROUPS // P)
QROWS = [min(P, GROUPS - q * P) for q in range(QUADS)]
HIDDEN = 4 * D
EPS = 1e-5
PACE = round(E / N)
SLACK = 2
READY = -(-FIRST_N * J * PACE // GROUP) + SLACK
SPREAD = 12
SLOTS = 8
AHEAD = 6


def is_loop(i):
    return not isinstance(i, int)


class Steps:

    def __init__(self, unroll, head):
        self.unroll, self.head = unroll, head

    def item(self, i, k):
        return i * self.unroll + k

    def done(self, i, k, per=1):
        return (i * self.unroll + (k + 1)) * per

    def landed(self, i, k, slots, per=16):
        return (i * (self.unroll // slots) + (k // slots + 1)) * per

    def first(self, i, k, slots):
        return not is_loop(i) and k < slots

    def reuse(self, eng, sem, i, k, slots, per=1):
        if not self.first(i, k, slots):
            eng.wait_ge(sem, (i * self.unroll + (k - slots + 1)) * per)

    def run(self, eng, count, stages, beside=lambda t: None, between=lambda: None):
        lags = [lag for lag, _ in stages]
        whole = (count - 1 + min(min(lags), 0) - self.head) // self.unroll

        def step(i, t):
            for lag, stage in stages:
                if is_loop(i) or 0 <= t - lag < count:
                    stage(i, t - lag)

        for t in range(min(min(lags), 0), self.head):
            step(0, t)
            beside(t)
        between()
        with eng.Fori(0, whole) as i:
            for s in range(self.unroll):
                step(i, self.head + s)
        for t in range(self.head + self.unroll * whole, count + max(lags)):
            step(0, t)


def run_together(eng, edge_stages, node_stages):
    lags = [lag for lag, _ in edge_stages] + [0]
    head = 2 * PACE
    whole = (GROUPS - 1 + min(lags) - head) // PACE

    def place(hop):
        return READY + 1 + (hop if hop < 0 else hop * SPREAD // HOPS)

    def step(i, t):
        for lag, stage in edge_stages:
            if is_loop(i) or 0 <= t - lag < GROUPS:
                stage(i, t - lag)
        for hop, stage in node_stages:
            batch, off = divmod(t - place(hop), PACE)
            if off == 0 and 0 <= batch < BATCHES:
                stage(i, batch)

    for t in range(min(lags), head):
        step(0, t)
    with eng.Fori(0, whole) as i:
        for s in range(PACE):
            step(i, head + s)
    for t in range(head + PACE * whole, PACE * (BATCHES - 1) + place(HOPS) + 1):
        step(0, t)


HOPS = 14


def after(eng, turn, sem, value):
    eng.wait_ge(sem, value)
    eng.sem_inc(turn, 1)


def spread(ap, shape):
    return ap.broadcast_to(shape)


def build(nc, x, src, dst, edge, Wm, bm, Wu, bu, gamma, beta, g1, b1ln, Wc, bconv, g2, b2ln, W1, b1, W2, b2, out):
    ctx = ExitStack()
    sp, pool, act, pe, dve = nc.sync, nc.gpsimd, nc.scalar, nc.tensor, nc.vector
    with ctx:
        def sb(name, shape, dt=F32, where=ctx):
            return where.enter_context(nc.sbuf_tensor(name, shape, dt))

        def ps(name, shape, where):
            return where.enter_context(nc.psum_tensor(name, shape, F32))

        class Sems:

            def __init__(self, phase, name):
                self.phase, self.name, self.nums = phase, name, []

            def __call__(self, name):
                s = self.phase.enter_context(nc.semaphore(self.name + name))
                self.nums.append(s.num)
                return s

            def join(self):
                nums = sorted(self.nums)
                starts = [n for n in nums if n - 1 not in nums]
                for lo in starts:
                    hi = next(n for n in nums if n >= lo and n + 1 not in nums)
                    nc.all_engine_barrier(sems_to_clear=range(lo, hi + 1))

        table0 = nc.dram_tensor("table0", (N, D), F32).ap()
        table1 = nc.dram_tensor("table1", (N, D), F32).ap()
        x1_dram = nc.dram_tensor("x1_dram", (N, D), F32).ap()

        sums = sb("sums", [P, SUMS])
        row = sb("row", [1, SUMS])
        rel = sb("rel", [P, GROUPS, J])
        srci = sb("srci", [P, GROUPS, J], I32)
        least = sb("least", [P, GROUPS])
        base_f = sb("base_f", [1, GROUPS])
        base_i = sb("base_i", [1, GROUPS], I32)
        win0 = sb("win0", [P, WINDOW])
        win = sb("win", [P, WINDOW])
        choice = sb("choice", [1, 2], I32)
        ident = sb("ident", [P, P])
        ones_row = sb("ones_row", [1, P])
        ones_bf = sb("ones_bf", [P, 1], BF16)
        wm = sb("wm", [P, 2, D])
        wu = sb("wu", [P, 2, D])
        wc = sb("wc", [P, D])
        dinv = sb("dinv", [P, BATCHES, J])
        vec = sb("vec", [P, 6])
        bcv = sb("bcv", [P, 7, D])
        b2_row = sb("b2_row", [1, D])
        table_of = sb("table_of", [1, 2])
        one_eps = sb("one_eps", [P, 2])
        GA, BE, BCV, BU, BM, G1, B1 = range(7)

        def rows_of(t, start, part):
            return t[bass.ds(start, part * J), :].rearrange("(p j) d -> p j d", j=J)

        def first_node(b):
            return 0 if isinstance(b, int) and b == 0 else b * GROUP - (GROUP - FIRST_N * J)

        def edges_of(t, g, part):
            return rows_of(t, g * GROUP, part)

        def batch_of(t, b, part):
            return rows_of(t, first_node(b), part)

        def nodes_of(t, b, part):
            return t[:, bass.ds(first_node(b), part * J)].rearrange("d (p j) -> d j p", j=J)

        def part_of(i, k):
            return FIRST_N if not is_loop(i) and k == 0 else P

        with ExitStack() as ph:
            ids = sb("ids", [P, 2, QUADS, GROUP], I32, ph)
            idf = sb("idf", [P, 2, QUADS, GROUP], F32, ph)
            lo = sb("lo", [P, QUADS], F32, ph)
            hi = sb("hi", [P, QUADS], F32, ph)
            lo_bc = sb("lo_bc", [P, QUADS, P], F32, ph)
            spanT = sb("spanT", [QUADS, 1], F32, ph)
            flags = sb("flags", [1, 4], F32, ph)
            span_i = sb("span_i", [1, 1], I32, ph)
            due_i = sb("due_i", [1, PACE * BATCHES], I32, ph)
            due = sb("due", [1, PACE * BATCHES], F32, ph)
            xb = sb("xb", [P, 8, J, D], F32, ph)
            xT = sb("xT", [P, 2, J, P], F32, ph)
            tb = sb("tb", [P, 4, J, D], F32, ph)
            vrows = sb("vrows", [6, D], F32, ph)
            win_i = sb("win_i", [P, WINDOW], I32, ph)
            ps_t = [ps(f"ps_t{s}", [P, J, P], ph) for s in range(2)]
            ps_x = [ps(f"ps_x{s}", [P, J, P], ph) for s in range(2)]
            ps_m = [ps(f"ps_m{s}", [P, J, D], ph) for s in range(2)]
            ps_s = ps("ps_s", [P, GROUP], ph)

            sem = Sems(ph, "prep_")
            ids_in, weights_in, early_in = [sem(f"ids_in{w}") for w in range(2)], sem("weights_in"), sem("early_in")
            ident_ok, iota_ok, const_ok, zero_ok = sem("ident_ok"), sem("iota_ok"), sem("const_ok"), sem("zero_ok")
            idf_ok, lohi_ok, lobc_ok, rel_ok = sem("idf_ok"), sem("lohi_ok"), sem("lobc_ok"), sem("rel_ok")
            id_t, id_ev, small_t, small_ev = sem("id_t"), sem("id_ev"), sem("small_t"), sem("small_ev")
            flag_ok, srcf_ok = sem("flag_ok"), sem("srcf_ok")
            x_in = [sem(f"x_in{s}") for s in range(8)]
            x_t, x_c, x_m, x_b = sem("x_t"), sem("x_c"), sem("x_m"), sem("x_b")
            tab_out = [sem(f"tab_out{s}") for s in range(4)]

            def as_row(t):
                return t.rearrange("(a n) -> a n", a=1)

            late = [(wu[:], Wu.rearrange("(t p) n -> p t n", p=P)), (wc[:], Wc),
                    (bcv[:, GA, :], as_row(gamma).broadcast_to([P, D])),
                    (bcv[:, BE, :], as_row(beta).broadcast_to([P, D])),
                    (bcv[:, BCV, :], as_row(bconv).broadcast_to([P, D])),
                    (bcv[:, BU, :], as_row(bu).broadcast_to([P, D])),
                    (bcv[:, G1, :], as_row(g1).broadcast_to([P, D])),
                    (bcv[:, B1, :], as_row(b1ln).broadcast_to([P, D])),
                    (vrows[0:1, :], as_row(g2)), (vrows[1:2, :], as_row(b2ln)),
                    (vrows[2:6, :], b1.rearrange("(q n) -> q n", n=D)), (b2_row[:], as_row(b2))]
            assert len(late) <= 12
            flat = [dst, src]
            EVAC = [(w, q) for w in range(2) for q in range(QUADS)]

            def tiles_beside(t):
                return [n for n in range(2 * QUADS) if 2 + min(n, QUADS + (n - QUADS) // 2) == t]

            st = Steps(8, head=8)

            with nc.Block() as block:
                @block.sync
                def _(_):
                    def load(i, k):
                        part = part_of(i, k)
                        st.reuse(sp, x_t, i, k, 8)
                        sp.dma_start(xb[0:part, k % 8], batch_of(x, st.item(i, k), part)).then_inc(x_in[k % 8], 16)

                    def store(i, k):
                        part = part_of(i, k)
                        sp.wait_ge(x_b, st.done(i, k))
                        sp.dma_start(batch_of(table0, st.item(i, k), part), tb[0:part, k % 4]).then_inc(tab_out[k % 4], 16)

                    st.run(sp, BATCHES, [(-6, load), (1, store)])
                    for s in range(4):
                        sp.wait_ge(tab_out[s], 16 * len(range(s, BATCHES, 4)))

                @block.gpsimd
                def _(_):
                    pool.memset(ident[:], 0.0).then_inc(ident_ok, 1)
                    pool.wait_ge(ident_ok, 1)
                    pool.affine_select(out=ident[:], in_=ident[:], compare_op=ALU.not_equal, fill=1.0, base=0,
                                       pattern=[[-1, P]], channel_multiplier=1).then_inc(ident_ok, 1)
                    pool.iota(win_i[:], pattern=[[1, WINDOW]], base=0, channel_multiplier=0).then_inc(iota_ok, 1)
                    pool.iota(due_i[:], pattern=[[GROUP, BATCHES], [0, PACE]], base=FIRST_N * J, channel_multiplier=0
                              ).then_inc(iota_ok, 1)
                    pool.wait_ge(ids_in[1], 16 * 4)
                    pool.tensor_copy(idf[:, 1, 0:QUADS - 1, :], ids[:, 1, 0:QUADS - 1, :]).then_inc(srcf_ok, 1)
                    pool.tensor_copy(idf[0:QROWS[-1], 1, QUADS - 1, :], ids[0:QROWS[-1], 1, QUADS - 1, :]
                                     ).then_inc(srcf_ok, 1)
                    pool.memset(row[:], 0.0).then_inc(zero_ok, 1)
                    pool.memset(sums[:], 0.0).then_inc(zero_ok, 1)
                    pool.wait_ge(rel_ok, 1)
                    tail = rel[:, GROUPS - 1, :]
                    pool.affine_select(out=tail, in_=tail, compare_op=ALU.is_ge, fill=-1.0, base=TAIL_E - 1,
                                       pattern=[[0, J]], channel_multiplier=-1).then_inc(rel_ok, 1)

                @block.scalar
                def _(_):
                    short = E - (GROUPS - 1) * GROUP
                    r = QROWS[-1] - 1
                    whole = QUADS - 1
                    for w in range(2):
                        act.dma_start(ids[:, w, 0:whole, :], flat[w][0:whole * P * GROUP]
                                      .rearrange("(q g e) -> g q e", g=P, e=GROUP)).then_inc(ids_in[w], 16)
                        act.dma_start(ids[0:r, w, whole, :], flat[w][whole * P * GROUP:(whole * P + r) * GROUP]
                                      .rearrange("(g e) -> g e", e=GROUP)).then_inc(ids_in[w], 16)
                        act.dma_start(ids[r:r + 1, w, whole, 0:short], as_row(flat[w][E - short:E])).then_inc(ids_in[w], 16)
                        act.dma_start(ids[r:r + 1, w, whole, short:GROUP],
                                      as_row(flat[w][E - (GROUP - short):E])).then_inc(ids_in[w], 16)
                        if w == 0:
                            act.dma_start(wm[:], Wm.rearrange("(t p) n -> p t n", p=P)).then_inc(early_in, 16)
                            act.dma_start(bcv[:, BM, :], as_row(bm).broadcast_to([P, D])).then_inc(early_in, 16)

                    def copy_x(i, k):
                        part = part_of(i, k)
                        st.reuse(act, x_m, i, k, 2)
                        act.wait_ge(x_t, st.done(i, k))
                        act.copy(xT[:, k % 2, :, 0:part], ps_x[k % 2][:, :, 0:part]).then_inc(x_c, 1)

                    def weights(t):
                        for to, what in late[2 * (t - 2):2 * (t - 1)] if t >= 2 else []:
                            act.dma_start(to, what).then_inc(weights_in, 16)

                    st.run(act, BATCHES, [(0, copy_x)], beside=weights)

                @block.tensor
                def _(_):
                    pe.wait_ge(ident_ok, 2)
                    pe.wait_ge(early_in, 32)

                    def transpose_x(i, k):
                        part = part_of(i, k)
                        pe.wait_ge(x_in[k % 8], st.landed(i, k, 8))
                        st.reuse(pe, x_c, i, k, 2)
                        for j in range(J):
                            last = pe.transpose(ps_x[k % 2][:, j, 0:part], xb[0:part, k % 8, j, :], ident[0:part, 0:part])
                        last.then_inc(x_t, 1)

                    def times_wm(i, k):
                        part = part_of(i, k)
                        pe.wait_ge(x_c, st.done(i, k))
                        st.reuse(pe, x_b, i, k, 2)
                        for j in range(J):
                            last = pe.matmul(ps_m[k % 2][0:part, j, :], xT[:, k % 2, j, 0:part], wm[:, 0, :],
                                             start=True, stop=True)
                        last.then_inc(x_m, 1)

                    def index_tiles(t):
                        for n in tiles_beside(t):
                            w, q = EVAC[n]
                            if w == 0:
                                pe.wait_ge(lobc_ok, q + 1)
                                if q >= 1:
                                    pe.wait_ge(small_ev, q)
                                pe.transpose(ps_s[:, 0:P], lo_bc[:, q, :], ident[:]).then_inc(small_t, 1)
                            if n >= 2:
                                pe.wait_ge(id_ev, n - 1)
                            if n == QUADS:
                                pe.wait_ge(srcf_ok, 2)
                            r = QROWS[q]
                            view = idf[0:r, w, q, :].rearrange("g (p j) -> g j p", j=J)
                            for j in range(J):
                                last = pe.transpose(ps_t[n % 2][:, j, 0:r], view[:, j, :], ident[0:r, 0:r])
                            last.then_inc(id_t, 1)

                    def widest():
                        pe.wait_ge(lobc_ok, QUADS + 1)
                        pe.wait_ge(small_ev, QUADS)
                        pe.transpose(ps_s[0:QUADS, 0:P], hi[:], ident[:]).then_inc(small_t, 1)
                        pe.wait_ge(small_ev, QUADS + 1)
                        pe.transpose(ps_s[0:1, 0:QUADS], spanT[:], ident[0:QUADS, 0:QUADS]).then_inc(small_t, 1)

                    st.run(pe, BATCHES, [(0, transpose_x), (1, times_wm)], beside=index_tiles, between=widest)
                    pe.wait_ge(weights_in, 16 * len(late))
                    pe.wait_ge(small_ev, QUADS + 2)
                    pe.transpose(ps_s[:, 0:6], vrows[:], ident[0:6, 0:6]).then_inc(small_t, 1)

                @block.vector
                def _(_):
                    dve.memset(ones_row[:], 1.0).then_inc(const_ok, 1)
                    dve.memset(ones_bf[:], 1.0).then_inc(const_ok, 1)
                    dve.memset(one_eps[:, 0:1], 1.0).then_inc(const_ok, 1)
                    dve.memset(one_eps[:, 1:2], EPS).then_inc(const_ok, 1)
                    dve.memset(lo[:], 0.0).then_inc(const_ok, 1)
                    dve.memset(hi[:], 0.0).then_inc(const_ok, 1)
                    dve.wait_ge(iota_ok, 2)
                    dve.tensor_copy(win0[:], win_i[:]).then_inc(const_ok, 1)
                    dve.tensor_copy(win[:], win_i[:]).then_inc(const_ok, 1)
                    dve.tensor_copy(due[:], due_i[:]).then_inc(const_ok, 1)
                    dve.wait_ge(const_ok, 9)
                    dve.wait_ge(ids_in[0], 16 * 4)
                    dve.tensor_copy(idf[:, 0, 0:QUADS - 1, :], ids[:, 0, 0:QUADS - 1, :]).then_inc(idf_ok, 1)
                    dve.tensor_copy(idf[0:QROWS[-1], 0, QUADS - 1, :], ids[0:QROWS[-1], 0, QUADS - 1, :]
                                    ).then_inc(idf_ok, 1)
                    dve.wait_ge(idf_ok, 2)
                    for q0, q1 in ((0, QUADS - 1), (QUADS - 1, QUADS)):
                        r = QROWS[q0]
                        dve.tensor_reduce(lo[0:r, q0:q1], idf[0:r, 0, q0:q1, :], AX.X, ALU.min).then_inc(lohi_ok, 1)
                        dve.tensor_reduce(hi[0:r, q0:q1], idf[0:r, 0, q0:q1, :], AX.X, ALU.max).then_inc(lohi_ok, 1)
                    dve.wait_ge(lohi_ok, 4)
                    for q in range(QUADS):
                        dve.tensor_copy(lo_bc[:, q, :], spread(lo[:, q:q + 1], [P, P])).then_inc(lobc_ok, 1)
                    dve.tensor_tensor(hi[:], hi[:], lo[:], ALU.subtract).then_inc(lobc_ok, 1)
                    dve.wait_ge(early_in, 32)

                    def table_rows(i, k):
                        part = part_of(i, k)
                        dve.wait_ge(x_m, st.done(i, k))
                        if not st.first(i, k, 4):
                            dve.wait_ge(tab_out[k % 4], st.landed(i, k - 4, 4))
                        dve.tensor_tensor(tb[0:part, k % 4], ps_m[k % 2][0:part],
                                          spread(bcv[0:part, BM:BM + 1, :], [part, J, D]), ALU.add).then_inc(x_b, 1)

                    def index_tiles(t):
                        for n in tiles_beside(t):
                            w, q = EVAC[n]
                            if w == 0:
                                dve.wait_ge(small_t, q + 1)
                                dve.tensor_copy(least[:, q * P:q * P + QROWS[q]], ps_s[:, 0:QROWS[q]]
                                                ).then_inc(small_ev, 1)
                            dve.wait_ge(id_t, n + 1)
                            to = (rel, srci)[w][:, q * P:q * P + QROWS[q], :].rearrange("p g j -> p j g")
                            dve.tensor_copy(to, ps_t[n % 2][:, :, 0:QROWS[q]]).then_inc(id_ev, 1)

                    def conditions():
                        dve.wait_ge(small_t, QUADS + 1)
                        dve.tensor_reduce(spanT[:], ps_s[0:QUADS, 0:P], AX.X, ALU.max).then_inc(small_ev, 1)
                        dve.wait_ge(small_ev, QUADS)
                        dve.wait_ge(id_ev, len(EVAC))
                        dve.tensor_tensor(rel[:], rel[:], spread(least[:].unsqueeze(2), [P, GROUPS, J]),
                                          ALU.subtract).then_inc(rel_ok, 1)
                        dve.tensor_copy(base_f[:], least[0:1, :]).then_inc(flag_ok, 1)
                        dve.tensor_copy(base_i[:], least[0:1, :]).then_inc(flag_ok, 1)
                        late_by = due[:, 0:GROUPS - READY]
                        dve.tensor_tensor(late_by, late_by, least[0:1, READY:GROUPS], ALU.subtract).then_inc(flag_ok, 1)
                        dve.wait_ge(flag_ok, 3)
                        dve.tensor_reduce(flags[:, 1:2], late_by, AX.X, ALU.max).then_inc(flag_ok, 1)
                        dve.wait_ge(small_t, QUADS + 2)
                        dve.tensor_reduce(flags[:, 0:1], ps_s[0:1, 0:QUADS], AX.X, ALU.max).then_inc(small_ev, 1)
                        dve.wait_ge(small_ev, QUADS + 2)
                        dve.wait_ge(flag_ok, 4)
                        dve.tensor_scalar(span_i[:], flags[:, 0:1], float(WINDOW), None, ALU.add).then_inc(flag_ok, 1)
                        dve.tensor_scalar(flags[:, 2:3], flags[:, 0:1], float(WINDOW), None, ALU.is_lt).then_inc(flag_ok, 1)
                        dve.tensor_scalar(flags[:, 3:4], flags[:, 1:2], 0.0, None, ALU.is_le).then_inc(flag_ok, 1)
                        dve.wait_ge(flag_ok, 7)
                        dve.tensor_scalar(choice[:, 0:1], span_i[:], WINDOW.bit_length() - 1, None,
                                          ALU.arith_shift_right).then_inc(flag_ok, 1)
                        dve.tensor_tensor(choice[:, 1:2], flags[:, 2:3], flags[:, 3:4], ALU.mult).then_inc(flag_ok, 1)

                    st.run(dve, BATCHES, [(1, table_rows)], beside=index_tiles, between=conditions)
                    dve.wait_ge(small_t, QUADS + 3)
                    dve.tensor_copy(vec[:], ps_s[:, 0:6]).then_inc(small_ev, 1)

            sem.join()

        def edge_stages(layer, ph, sem, se):
            L = sem.name
            table = (table0, table1)[layer]
            idx = sb(L + "idx", [P, SLOTS, J], I32, ph)
            got = sb(L + "got", [P, SLOTS, J, D], F32, ph)
            hot = sb(L + "hot", [P, 4, J, WINDOW], F32, ph)
            banks = [ps(L + f"window{s}", [P, 2 * WINDOW], ph) for s in range(2)]
            win_sum = [bank[:, 0:WINDOW] for bank in banks]
            win_cnt = [bank[0:1, WINDOW:2 * WINDOW] for bank in banks]
            turn_pool, turn_act = sem("turn_pool"), sem("turn_act")
            got_in = [sem(f"got_in{s}") for s in range(SLOTS)]
            idx_ok, hot_ok, seg_ok, flushed = sem("idx_ok"), sem("hot_ok"), sem("seg_ok"), sem("flushed")
            counted = flushed
            if layer == 0:
                counted = sem("counted")
                ea = sb(L + "ea", [P, 4, J, D], F32, ph)
                eaT = sb(L + "eaT", [P, 2, J, P], F32, ph)
                msg = sb(L + "msg", [P, 4, J, D], F32, ph)
                ps_e = ps(L + "ps_e", [P, J, P], ph)
                ps_p = [ps(L + f"ps_p{s}", [P, J, D], ph) for s in range(2)]
                ea_in = [sem(f"ea_in{s}") for s in range(4)]
                ea_t, ea_c, pre_ok, add_ok, relu_ok = (sem(n) for n in ("ea_t", "ea_c", "pre_ok", "add_ok", "relu_ok"))
            got_used = add_ok if layer == 0 else seg_ok

            def gather(i, k):
                s = k % SLOTS
                if not se.first(i, k, SLOTS):
                    after(pool, turn_pool, got_used, se.done(i, k - SLOTS))
                after(pool, turn_pool, idx_ok, se.done(i, k))
                for j in range(J):
                    pool.indirect_dma_start(
                        out=got[:, s, j, :], out_offset=None, in_=table,
                        in_offset=bass.IndirectOffsetOnAxis(ap=idx[:, s, j:j + 1], axis=0)
                    ).then_inc(got_in[s], 16)

            def gathers_end():
                for s in range(SLOTS):
                    pool.wait_ge(got_in[s], 16 * J * len(range(s, GROUPS, SLOTS)))
                nums = [s.num for s in got_in]
                pool.dma_reset(range(min(nums), max(nums) + 1))

            def load_edges(i, k):
                part = TAIL_E if not is_loop(i) and k == GROUPS - 1 else P
                se.reuse(sp, ea_t, i, k, 4)
                sp.dma_start(ea[0:part, k % 4], edges_of(edge, se.item(i, k), part)).then_inc(ea_in[k % 4], 16)

            def lay_indices(i, k):
                s = k % SLOTS
                if not se.first(i, k, SLOTS):
                    after(act, turn_act, got_in[s], se.landed(i, k - SLOTS, SLOTS, 16 * J))
                act.copy(idx[:, s, :], srci[:, bass.ds(se.item(i, k), 1), :].rearrange("p a j -> p (a j)")
                         ).then_inc(idx_ok, 1)

            def copy_edges(i, k):
                se.reuse(act, pre_ok, i, k, 2)
                act.wait_ge(ea_t, se.done(i, k))
                act.copy(eaT[:, k % 2], ps_e[:]).then_inc(ea_c, 1)

            def relu(i, k):
                act.wait_ge(add_ok, se.done(i, k))
                act.activation(msg[:, k % 4], msg[:, k % 4], ACT.Relu).then_inc(relu_ok, 1)

            def transpose_edges(i, k):
                pe.wait_ge(ea_in[k % 4], se.landed(i, k, 4))
                se.reuse(pe, ea_c, i, k, 1)
                for j in range(J):
                    last = pe.transpose(ps_e[:, j, :], ea[:, k % 4, j, :], ident[:])
                last.then_inc(ea_t, 1)

            def times_wm(i, k):
                pe.wait_ge(ea_c, se.done(i, k))
                se.reuse(pe, add_ok, i, k, 2)
                for j in range(J):
                    last = pe.matmul(ps_p[k % 2][:, j, :], eaT[:, k % 2, j, :], wm[:, 1, :], start=True, stop=True)
                last.then_inc(pre_ok, 1)

            def segment(i, k):
                pe.wait_ge(hot_ok, se.done(i, k))
                if layer == 0:
                    pe.wait_ge(relu_ok, se.done(i, k))
                else:
                    pe.wait_ge(got_in[k % SLOTS], se.landed(i, k, SLOTS, 16 * J))
                se.reuse(pe, flushed, i, k, 2)
                if layer == 0:
                    se.reuse(pe, counted, i, k, 2)
                for j in range(J):
                    rows = msg[:, k % 4, j, :] if layer == 0 else got[:, k % SLOTS, j, :]
                    last = pe.matmul(win_sum[k % 2], rows, hot[:, k % 4, j, :], start=(j == 0), stop=(j == J - 1))
                if layer == 0:
                    ones = hot[:, k % 4].bitcast(BF16).rearrange("p j (w h) -> p j w h", h=2)
                    for j in range(J):
                        last = pe.matmul(win_cnt[k % 2], ones_bf[:], ones[:, j, :, 1], start=(j == 0), stop=(j == J - 1))
                last.then_inc(seg_ok, 1)

            def one_hot(i, k):
                se.reuse(dve, seg_ok, i, k, 4)
                at = rel[:, bass.ds(se.item(i, k), 1), :].rearrange("p a j -> p (a j)").unsqueeze(2)
                dve.tensor_tensor(hot[:, k % 4], spread(at, [P, J, WINDOW]), spread(win[:].unsqueeze(1), [P, J, WINDOW]),
                                  ALU.is_equal).then_inc(hot_ok, 1)

            def add(i, k):
                s = k % SLOTS
                dve.wait_ge(got_in[s], se.landed(i, k, SLOTS, 16 * J))
                dve.wait_ge(pre_ok, se.done(i, k))
                se.reuse(dve, seg_ok, i, k, 4)
                dve.tensor_tensor(msg[:, k % 4], ps_p[k % 2][:], got[:, s], ALU.add).then_inc(add_ok, 1)

            def flush(i, k):
                first = dve.value_load(base_i[0:1, bass.ds(se.item(i, k), 1)], min_val=0, max_val=N)
                dve.wait_ge(seg_ok, se.done(i, k))
                se.reuse(dve, flushed, i, k, 1)
                to = sums[:, bass.ds(first, WINDOW)]
                dve.tensor_tensor(to, win_sum[k % 2], to, ALU.add).then_inc(flushed, 1)
                if layer == 0:
                    se.reuse(dve, counted, i, k, 1)
                    to = row[:, bass.ds(first, WINDOW)]
                    dve.tensor_tensor(to, win_cnt[k % 2], to, ALU.add).then_inc(counted, 1)

            if layer == 0:
                stages = {"sp": [(0, load_edges)], "pool": [(0, gather)],
                          "act": [(-AHEAD, lay_indices), (0, copy_edges), (1, relu)],
                          "pe": [(0, transpose_edges), (1, times_wm), (2, segment)],
                          "dve": [(0, one_hot), (1, add), (2, flush)]}
            else:
                stages = {"sp": [], "pool": [(0, gather)], "act": [(-AHEAD, lay_indices)],
                          "pe": [(0, segment)], "dve": [(-1, one_hot), (1, flush)]}
            return stages, gathers_end, flushed, counted, seg_ok

        def normalise(ph, sem, n):
            L = sem.name + f"n{n}_"
            bn = sb(L + "bn", [P, J, 6], F32, ph)
            mv = sb(L + "mv", [P, J, 2], F32, ph)
            sd = sb(L + "sd", [P, J], F32, ph)
            rs = sb(L + "rs", [P, J], F32, ph)
            return bn, mv, sd, rs, [sem(f"{w}{n}") for w in ("bn", "mv", "sd", "rs")]

        def stats(st, turn_dve, norm, value, ready, used, i, k):
            bn, mv, sd, rs, (bn_ok, mv_ok, sd_ok, rs_ok) = norm
            part = part_of(i, k)
            dve.wait_ge(ready, st.done(i, k))
            st.reuse(dve, mv_ok, i, k, 1)
            for j in range(J):
                last = dve.bn_stats(bn[0:part, j, :], value[0:part, j, :])
            last.then_inc(bn_ok, 1)
            st.reuse(dve, used, i, k, 1)
            after(dve, turn_dve, bn_ok, st.done(i, k))
            for j in range(J):
                last = dve.bn_aggr(mv[0:part, j, :], bn[0:part, j, :])
            last.then_inc(mv_ok, 1)

        def root(st, norm, i, k):
            bn, mv, sd, rs, (bn_ok, mv_ok, sd_ok, rs_ok) = norm
            part = part_of(i, k)
            st.reuse(act, rs_ok, i, k, 1, 4)
            act.wait_ge(mv_ok, st.done(i, k))
            act.activation(sd[0:part], mv[0:part, :, 1], ACT.Sqrt, bias=one_eps[0:part, 1:2]).then_inc(sd_ok, 1)

        def inverse(st, norm, used, i, k):
            bn, mv, sd, rs, (bn_ok, mv_ok, sd_ok, rs_ok) = norm
            part = part_of(i, k)
            dve.wait_ge(sd_ok, st.done(i, k))
            st.reuse(dve, used, i, k, 1)
            inverse_root(st, i, k, mv[0:part, :, 1], EPS, sd[0:part], rs[0:part], rs[0:part], rs_ok)

        def inverse_root(st, i, k, value, plus, root_of, y, to, ok):
            def step(n):
                dve.wait_ge(ok, st.item(i, k) * 4 + n)

            dve.reciprocal(y, root_of).then_inc(ok, 1)
            step(1)
            dve.scalar_tensor_tensor(root_of, value, plus, y, ALU.add, ALU.mult).then_inc(ok, 1)
            step(2)
            dve.scalar_tensor_tensor(root_of, root_of, -0.5, y, ALU.mult, ALU.mult).then_inc(ok, 1)
            step(3)
            dve.scalar_tensor_tensor(to, root_of, 1.5, y, ALU.add, ALU.mult).then_inc(ok, 1)
            step(4)

        def preload(function):
            at = 0 if function == ACT.Gelu else 1
            act.activation(table_of[:, at:at + 1], one_eps[0:1, 0:1], function)

        def scaled(norm, to, value, part):
            bn, mv, sd, rs, _ = norm
            for j in range(J):
                last = dve.tensor_scalar(to[0:part, j, :], value[0:part, j, :], mv[0:part, j, 0:1], rs[0:part, j:j + 1],
                                         ALU.subtract, ALU.mult)
            return last

        def node_stages_0(ph, sem, st, summed):
            L = sem.name
            xb = sb(L + "xb", [P, J, D], F32, ph)
            xT = sb(L + "xT", [P, J, P], F32, ph)
            aS = sb(L + "aS", [P, J, P], F32, ph)
            cr = sb(L + "cr", [1, GROUP], F32, ph)
            xw = sb(L + "xw", [P, J, D], F32, ph)
            dd = sb(L + "dd", [P, 4, J], F32, ph)
            ic = sb(L + "ic", [P, J], F32, ph)
            h = sb(L + "h", [P, J, D], F32, ph)
            x1 = sb(L + "x1", [P, J, D], F32, ph)
            nrm = sb(L + "nrm", [P, J, D], F32, ph)
            g = sb(L + "g", [P, J, D], F32, ph)
            u = sb(L + "u", [P, J, D], F32, ph)
            ps_t = ps(L + "ps_t", [P, J, P], ph)
            ps_x = ps(L + "ps_x", [P, J, D], ph)
            ps_a = ps(L + "ps_a", [P, J, D], ph)
            turn_act, turn_dve = sem("node_turn_act"), sem("node_turn_dve")
            c = {n: sem("node_" + n) for n in ("x_in", "cr", "aS", "x_t", "cnt", "x_c", "dd", "mx", "dinv", "ic", "px", "pa", "xw",
                                               "h", "t1", "t2", "s", "x1", "x1_out", "nrm", "ng", "gelu", "u",
                                               "u_out", "u_t", "init")}
            norm = [normalise(ph, sem, n) for n in range(3)]

            def load_x(i, k):
                part = part_of(i, k)
                st.reuse(sp, c["s"], i, k, 1)
                sp.dma_start(xb[0:part], batch_of(x, st.item(i, k), part)).then_inc(c["x_in"], 16)

            def copy_counts(i, k):
                part = part_of(i, k)
                summed(act, turn_act, i, k)
                if not st.first(i, k, 1):
                    after(act, turn_act, c["cnt"], st.done(i, k - 1))
                act.copy(cr[:, 0:part * J], row[:, bass.ds(first_node(st.item(i, k)), part * J)]).then_inc(c["cr"], 1)

            def transpose_x(i, k):
                part = part_of(i, k)
                pe.wait_ge(c["x_in"], st.done(i, k, 16))
                st.reuse(pe, c["init"], i, k, 1)
                for j in range(J):
                    last = pe.transpose(ps_t[:, j, 0:part], xb[0:part, j, :], ident[0:part, 0:part])
                last.then_inc(c["x_t"], 1)

            def copy_x(i, k):
                part = part_of(i, k)
                st.reuse(act, c["px"], i, k, 1)
                act.wait_ge(c["x_t"], st.done(i, k))
                act.copy(xT[:, :, 0:part], ps_t[:, :, 0:part]).then_inc(c["x_c"], 1)

            def product_x(i, k):
                part = part_of(i, k)
                pe.wait_ge(c["x_c"], st.done(i, k))
                st.reuse(pe, c["mx"], i, k, 1, 2)
                for j in range(J):
                    last = pe.matmul(ps_x[0:part, j, :], xT[:, j, 0:part], wu[:, 0, :], start=True, stop=True)
                last.then_inc(c["px"], 1)

            def with_bias(i, k):
                part = part_of(i, k)
                dve.wait_ge(c["px"], st.done(i, k))
                st.reuse(dve, c["h"], i, k, 1)
                dve.tensor_tensor(xw[0:part], ps_x[0:part], spread(bcv[0:part, BU:BU + 1, :], [part, J, D]),
                                  ALU.add).then_inc(c["xw"], 1)

            def copy_sums(i, k):
                part = part_of(i, k)
                summed(dve, turn_dve, i, k)
                st.reuse(dve, c["pa"], i, k, 1)
                dve.tensor_copy(aS[:, :, 0:part], nodes_of(sums, st.item(i, k), part)).then_inc(c["aS"], 1)

            def product_sums(i, k):
                part = part_of(i, k)
                pe.wait_ge(c["cr"], st.done(i, k))
                pe.wait_ge(c["xw"], st.done(i, k))
                counts = cr[:, 0:part * J].rearrange("a (p j) -> a j p", j=J)
                for j in range(J):
                    last = pe.matmul(ps_x[0:part, 0, j:j + 1], counts[:, j, :], ones_row[:, 0:1], start=True, stop=True)
                last.then_inc(c["cnt"], 1)
                pe.wait_ge(c["aS"], st.done(i, k))
                st.reuse(pe, c["h"], i, k, 1)
                for j in range(J):
                    last = pe.matmul(ps_a[0:part, j, :], aS[:, j, 0:part], wu[:, 1, :], start=True, stop=True)
                last.then_inc(c["pa"], 1)

            def update(i, k):
                part = part_of(i, k)
                dve.wait_ge(c["cnt"], st.done(i, k))
                st.reuse(dve, c["ic"], i, k, 1)
                st.reuse(dve, c["dinv"], i, k, 1, 4)
                dve.tensor_scalar(dd[0:part, 1, :], ps_x[0:part, 0, 0:J], 1.0, None, ALU.max).then_inc(c["mx"], 1)
                dve.tensor_copy(dd[0:part, 2, :], ps_x[0:part, 0, 0:J]).then_inc(c["mx"], 1)
                dve.wait_ge(c["mx"], st.done(i, k, 2))
                st.reuse(dve, c["h"], i, k, 1)
                dve.reciprocal(ic[0:part], dd[0:part, 1, :]).then_inc(c["ic"], 1)
                dve.wait_ge(c["ic"], st.done(i, k))
                dve.wait_ge(c["pa"], st.done(i, k))
                if not st.first(i, k, 1):
                    dve.wait_ge(c["x1"], st.done(i, k - 1))
                for j in range(J):
                    last = dve.scalar_tensor_tensor(h[0:part, j, :], ps_a[0:part, j, :], ic[0:part, j:j + 1],
                                                    xw[0:part, j, :], ALU.mult, ALU.add)
                last.then_inc(c["h"], 1)
                stats(st, turn_dve, norm[0], h, c["h"], c["t1"], i, k)

            def norm_root(n, i, k):
                root(st, norm[n], i, k)
                if n == 0:
                    part = part_of(i, k)
                    st.reuse(act, c["dinv"], i, k, 1, 4)
                    act.wait_ge(c["mx"], st.done(i, k, 2))
                    act.activation(dd[0:part, 0, :], dd[0:part, 2, :], ACT.Sqrt, bias=one_eps[0:part, 0:1]
                                   ).then_inc(c["dd"], 1)
                elif n == 2:
                    preload(ACT.Gelu)

            def inverse_count(i, k):
                part = part_of(i, k)
                dve.wait_ge(c["dd"], st.done(i, k))
                to = dinv[0:part, bass.ds(st.item(i, k), 1), :].rearrange("p a j -> p (a j)")
                inverse_root(st, i, k, dd[0:part, 2, :], 1.0, dd[0:part, 0, :], dd[0:part, 3, :], to, c["dinv"])

            def layer0_norm(i, k):
                part = part_of(i, k)
                bn, mv, sd, rs, (bn_ok, mv_ok, sd_ok, rs_ok) = norm[0]
                inverse(st, norm[0], c["t2"], i, k)
                for j in range(J):
                    last = dve.scalar_tensor_tensor(h[0:part, j, :], h[0:part, j, :], mv[0:part, j, 0:1],
                                                    bcv[0:part, GA, :], ALU.subtract, ALU.mult)
                last.then_inc(c["t1"], 1)
                dve.wait_ge(c["t1"], st.done(i, k))
                for j in range(J):
                    last = dve.scalar_tensor_tensor(h[0:part, j, :], h[0:part, j, :], rs[0:part, j:j + 1],
                                                    bcv[0:part, BE, :], ALU.mult, ALU.add)
                last.then_inc(c["t2"], 1)

            def layer0_relu(i, k):
                part = part_of(i, k)
                dve.wait_ge(c["t2"], st.done(i, k))
                dve.tensor_tensor(h[0:part], h[0:part], xb[0:part], ALU.add).then_inc(c["hx"], 1)
                dve.wait_ge(c["hx"], st.done(i, k))
                dve.scalar_tensor_tensor(h[0:part], h[0:part], 0.0, xb[0:part], ALU.max, ALU.add).then_inc(c["s"], 1)
                stats(st, turn_dve, norm[1], h, c["s"], c["x1"], i, k)

            c["hx"] = sem("node_hx")

            def first_norm(i, k):
                part = part_of(i, k)
                inverse(st, norm[1], c["x1"], i, k)
                if not st.first(i, k, 1):
                    dve.wait_ge(c["x1_out"], st.done(i, k - 1, 16))
                    dve.wait_ge(c["nrm"], st.done(i, k - 1))
                scaled(norm[1], x1, h, part).then_inc(c["x1"], 1)
                stats(st, turn_dve, norm[2], x1, c["x1"], c["nrm"], i, k)

            def second_norm(i, k):
                part = part_of(i, k)
                bn, mv, sd, rs, _ = norm[2]
                inverse(st, norm[2], c["nrm"], i, k)
                st.reuse(dve, c["gelu"], i, k, 1)
                for j in range(J):
                    last = dve.scalar_tensor_tensor(nrm[0:part, j, :], x1[0:part, j, :], mv[0:part, j, 0:1],
                                                    bcv[0:part, G1, :], ALU.subtract, ALU.mult)
                last.then_inc(c["ng"], 1)
                dve.wait_ge(c["ng"], st.done(i, k))
                for j in range(J):
                    last = dve.scalar_tensor_tensor(nrm[0:part, j, :], nrm[0:part, j, :], rs[0:part, j:j + 1],
                                                    bcv[0:part, B1, :], ALU.mult, ALU.add)
                last.then_inc(c["nrm"], 1)

            def store_x1(i, k):
                part = part_of(i, k)
                sp.wait_ge(c["x1"], st.done(i, k))
                sp.dma_start(batch_of(x1_dram, st.item(i, k), part), x1[0:part]).then_inc(c["x1_out"], 16)

            def gelu(i, k):
                part = part_of(i, k)
                st.reuse(act, c["u"], i, k, 1)
                act.wait_ge(c["nrm"], st.done(i, k))
                act.activation(g[0:part], nrm[0:part], ACT.Gelu).then_inc(c["gelu"], 1)
                preload(ACT.Sqrt)

            def scale_u(i, k):
                part = part_of(i, k)
                dve.wait_ge(c["gelu"], st.done(i, k))
                dve.wait_ge(c["dinv"], st.done(i, k, 4))
                if not st.first(i, k, 1):
                    dve.wait_ge(c["u_out"], st.done(i, k - 1, 16))
                    dve.wait_ge(c["u_t"], st.done(i, k - 1))
                at = dinv[0:part, bass.ds(st.item(i, k), 1), :].rearrange("p a j -> p (a j)").unsqueeze(2)
                dve.tensor_tensor(u[0:part], g[0:part], spread(at, [part, J, D]), ALU.mult).then_inc(c["u"], 1)

            def store_u(i, k):
                part = part_of(i, k)
                sp.wait_ge(c["u"], st.done(i, k))
                sp.dma_start(batch_of(table1, st.item(i, k), part), u[0:part]).then_inc(c["u_out"], 16)

            def transpose_u(i, k):
                part = part_of(i, k)
                pe.wait_ge(c["u"], st.done(i, k))
                pe.wait_ge(c["x_c"], st.done(i, k))
                for j in range(J):
                    last = pe.transpose(ps_t[:, j, 0:part], u[0:part, j, :], ident[0:part, 0:part])
                last.then_inc(c["u_t"], 1)

            def self_loop(i, k):
                part = part_of(i, k)
                after(act, turn_act, c["u_t"], st.done(i, k))
                act.copy(nodes_of(sums, st.item(i, k), part), ps_t[:, :, 0:part]).then_inc(c["init"], 1)

            def ended():
                sp.wait_ge(c["x1_out"], 16 * BATCHES)
                sp.wait_ge(c["u_out"], 16 * BATCHES)

            return {"sp": [(-5, load_x), (8, store_x1), (12, store_u)],
                    "pool": [],
                    "act": [(-3, copy_x), (0, copy_counts), (3, lambda i, k: norm_root(0, i, k)),
                            (6, lambda i, k: norm_root(1, i, k)), (8, lambda i, k: norm_root(2, i, k)),
                            (10, gelu), (13, self_loop)],
                    "pe": [(-4, transpose_x), (-2, product_x), (1, product_sums), (12, transpose_u)],
                    "dve": [(-1, with_bias), (0, copy_sums), (2, update), (4, layer0_norm), (5, layer0_relu),
                            (7, first_norm), (9, second_norm), (10, inverse_count), (11, scale_u)]}, ended

        def node_stages_1(ph, sem, st, summed):
            L = sem.name
            x1 = sb(L + "x1", [P, J, D], F32, ph)
            z = sb(L + "z", [P, J, D], F32, ph)
            aS = sb(L + "aS", [P, J, P], F32, ph)
            nrm = sb(L + "nrm", [P, J, D], F32, ph)
            zT = sb(L + "zT", [P, J, P], F32, ph)
            w1 = sb(L + "w1", [P, HIDDEN], F32, ph)
            w2 = sb(L + "w2", [P, J, D], F32, ph)
            fT = sb(L + "fT", [P, J, J, P], F32, ph)
            f = sb(L + "f", [P, J, D], F32, ph)
            o = sb(L + "o", [P, J, D], F32, ph)
            ps_z = ps(L + "ps_z", [P, J, D], ph)
            ps_t = ps(L + "ps_t", [P, J, P], ph)
            ps_f = [ps(L + f"ps_f{q}", [P, J, P], ph) for q in range(4)]
            ps_o = ps_z
            turn_dve = sem("node_turn_dve")
            e = {n: sem("node_" + n) for n in ("w", "x_in", "aS", "conv", "xb", "z", "nrm", "n_t", "zT", "up", "gelu",
                                               "down", "f", "s", "o", "out")}
            norm = [normalise(ph, sem, n) for n in range(2)]

            def weights():
                sp.dma_start(w1[:], W1).then_inc(e["w"], 16)
                sp.dma_start(w2[:], W2.rearrange("(q p) n -> p q n", p=P)).then_inc(e["w"], 16)

            def load_x1(i, k):
                part = part_of(i, k)
                st.reuse(sp, e["s"], i, k, 1)
                sp.dma_start(x1[0:part], batch_of(x1_dram, st.item(i, k), part)).then_inc(e["x_in"], 16)

            def copy_sums(i, k):
                part = part_of(i, k)
                summed(dve, turn_dve, i, k)
                st.reuse(dve, e["conv"], i, k, 1)
                dve.tensor_copy(aS[:, :, 0:part], nodes_of(sums, st.item(i, k), part)).then_inc(e["aS"], 1)
                dve.wait_ge(e["x_in"], st.done(i, k, 16))
                st.reuse(dve, e["nrm"], i, k, 1)
                dve.tensor_tensor(z[0:part], x1[0:part], spread(bcv[0:part, BCV:BCV + 1, :], [part, J, D]),
                                  ALU.add).then_inc(e["xb"], 1)

            def conv(i, k):
                part = part_of(i, k)
                pe.wait_ge(e["aS"], st.done(i, k))
                st.reuse(pe, e["f"], i, k, 1)
                for j in range(J):
                    last = pe.matmul(ps_z[0:part, j, :], aS[:, j, 0:part], wc[:], start=True, stop=True)
                last.then_inc(e["conv"], 1)

            def residual(i, k):
                part = part_of(i, k)
                dve.wait_ge(e["conv"], st.done(i, k))
                dve.wait_ge(e["xb"], st.done(i, k))
                for j in range(J):
                    at = dinv[0:part, bass.ds(st.item(i, k), 1), j]
                    last = dve.scalar_tensor_tensor(z[0:part, j, :], ps_z[0:part, j, :], at, z[0:part, j, :],
                                                    ALU.mult, ALU.add)
                last.then_inc(e["z"], 1)
                stats(st, turn_dve, norm[0], z, e["z"], e["nrm"], i, k)

            def first_root(i, k):
                root(st, norm[0], i, k)
                preload(ACT.Gelu)

            def norm2(i, k):
                part = part_of(i, k)
                inverse(st, norm[0], e["nrm"], i, k)
                st.reuse(dve, e["n_t"], i, k, 1)
                scaled(norm[0], nrm, z, part).then_inc(e["nrm"], 1)

            def transpose_n(i, k):
                part = part_of(i, k)
                pe.wait_ge(e["nrm"], st.done(i, k))
                st.reuse(pe, e["zT"], i, k, 1)
                for j in range(J):
                    last = pe.transpose(ps_t[:, j, 0:part], nrm[0:part, j, :], ident[0:part, 0:part])
                last.then_inc(e["n_t"], 1)

            def affine(i, k):
                part = part_of(i, k)
                act.wait_ge(e["n_t"], st.done(i, k))
                st.reuse(act, e["up"], i, k, 1, J)
                act.activation(zT[:, :, 0:part], ps_t[:, :, 0:part], ACT.Identity, bias=vec[:, 1:2], scale=vec[:, 0:1]
                               ).then_inc(e["zT"], 1)

            def up(i, k):
                part = part_of(i, k)
                pe.wait_ge(e["zT"], st.done(i, k))
                st.reuse(pe, e["gelu"], i, k, 1, J)
                for q in range(4):
                    pe.matmul(ps_f[q][:, :, 0:part], w1[:, q * P:(q + 1) * P], zT[:, :, 0:part],
                              start=True, stop=True).then_inc(e["up"], 1)

            def gelu_up(i, k):
                part = part_of(i, k)
                st.reuse(act, e["down"], i, k, 1)
                for q in range(4):
                    act.wait_ge(e["up"], st.item(i, k) * J + (q + 1))
                    act.activation(fT[:, q, :, 0:part], ps_f[q][:, :, 0:part], ACT.Gelu, bias=vec[:, 2 + q:3 + q]
                                   ).then_inc(e["gelu"], 1)

            def down(i, k):
                part = part_of(i, k)
                pe.wait_ge(e["z"], st.done(i, k))
                for j in range(J):
                    pe.matmul(ps_o[0:part, j, :], ones_row[:, 0:part], b2_row[:], start=True, stop=False)
                    if j == 0:
                        pe.wait_ge(e["gelu"], st.done(i, k, J))
                    for q in range(4):
                        last = pe.matmul(ps_o[0:part, j, :], fT[:, q, j, 0:part], w2[:, q, :], start=False, stop=(q == 3))
                last.then_inc(e["down"], 1)

            def gelu_down(i, k):
                part = part_of(i, k)
                act.wait_ge(e["down"], st.done(i, k))
                st.reuse(act, e["o"], i, k, 1)
                act.activation(f[0:part], ps_o[0:part], ACT.Gelu).then_inc(e["f"], 1)
                preload(ACT.Sqrt)

            def twice(i, k):
                part = part_of(i, k)
                dve.wait_ge(e["f"], st.done(i, k))
                dve.scalar_tensor_tensor(f[0:part], x1[0:part], 2.0, f[0:part], ALU.mult, ALU.add).then_inc(e["s"], 1)
                stats(st, turn_dve, norm[1], f, e["s"], e["o"], i, k)

            def norm3(i, k):
                part = part_of(i, k)
                inverse(st, norm[1], e["o"], i, k)
                if not st.first(i, k, 1):
                    dve.wait_ge(e["out"], st.done(i, k - 1, 16))
                scaled(norm[1], o, f, part).then_inc(e["o"], 1)

            def store(i, k):
                part = part_of(i, k)
                sp.wait_ge(e["o"], st.done(i, k))
                sp.dma_start(batch_of(out, st.item(i, k), part), o[0:part]).then_inc(e["out"], 16)

            def ended():
                sp.wait_ge(e["out"], 16 * BATCHES)

            def weights_ready():
                pe.wait_ge(e["w"], 32)

            return {"sp": [(-1, load_x1), (14, store)],
                    "pool": [],
                    "act": [(3, first_root), (6, affine), (8, gelu_up), (10, gelu_down),
                            (12, lambda i, k: root(st, norm[1], i, k))],
                    "pe": [(1, conv), (5, transpose_n), (7, up), (9, down)],
                    "dve": [(0, copy_sums), (2, residual), (4, norm2), (11, twice), (13, norm3)]}, \
                ended, weights, weights_ready

        def windows_reset(done):
            dve.tensor_copy(win[:], win0[:]).then_inc(done, 1)
            dve.tensor_copy(base_f[:], least[0:1, :]).then_inc(done, 1)
            dve.tensor_copy(base_i[:], least[0:1, :]).then_inc(done, 1)

        def node_part(layer, ph, sem, st, summed):
            if layer == 0:
                return node_stages_0(ph, sem, st, summed) + (lambda: None, lambda: None)
            return node_stages_1(ph, sem, st, summed)

        def together(layer):
            with ExitStack() as ph:
                sem = Sems(ph, f"both{layer}_")
                se, st = Steps(PACE, 2 * PACE), Steps(1, 2)
                stages, gathers_end, flushed, counted, seg_ok = edge_stages(layer, ph, sem, se)

                def summed(eng, turn, i, k):
                    groups = GROUPS if not is_loop(i) and k == BATCHES - 1 else (i + k) * PACE + READY
                    after(eng, turn, flushed if eng is dve else counted, groups)

                nodes, ended, weights, weights_ready = node_part(layer, ph, sem, st, summed)
                with nc.Block() as block:
                    @block.sync
                    def _(_):
                        weights()
                        run_together(sp, stages["sp"], nodes["sp"])
                        ended()

                    @block.gpsimd
                    def _(_):
                        se.run(pool, GROUPS, stages["pool"])
                        gathers_end()

                    @block.scalar
                    def _(_):
                        run_together(act, stages["act"], nodes["act"])

                    @block.tensor
                    def _(_):
                        weights_ready()
                        run_together(pe, stages["pe"], nodes["pe"])

                    @block.vector
                    def _(_):
                        run_together(dve, stages["dve"], nodes["dve"])

                sem.join()

        def apart(layer):
            with ExitStack() as ph:
                sem = Sems(ph, f"edges{layer}_")
                se = Steps(SLOTS, SLOTS)
                stages, gathers_end, flushed, counted, seg_ok = edge_stages(layer, ph, sem, se)
                moved = sem("moved")
                with nc.Fori(0, passes):
                    with nc.Block() as block:
                        @block.sync
                        def _(_):
                            if stages["sp"]:
                                se.run(sp, GROUPS, stages["sp"])

                        @block.gpsimd
                        def _(_):
                            se.run(pool, GROUPS, stages["pool"])
                            gathers_end()

                        @block.scalar
                        def _(_):
                            se.run(act, GROUPS, stages["act"])

                        @block.tensor
                        def _(_):
                            se.run(pe, GROUPS, stages["pe"])

                        @block.vector
                        def _(_):
                            se.run(dve, GROUPS, stages["dve"])
                            dve.wait_ge(seg_ok, GROUPS)
                            dve.tensor_scalar(base_f[:], base_f[:], float(WINDOW), float(N), ALU.add, ALU.min
                                              ).then_inc(moved, 1)
                            dve.tensor_scalar(win[:], win[:], float(WINDOW), None, ALU.add).then_inc(moved, 1)
                            dve.wait_ge(moved, 2)
                            dve.tensor_copy(base_i[:], base_f[:]).then_inc(moved, 1)

                    sem.join()

            with ExitStack() as ph:
                sem = Sems(ph, f"nodes{layer}_")
                st = Steps(1, 2)
                nodes, ended, weights, weights_ready = node_part(layer, ph, sem, st, lambda eng, turn, i, k: None)
                reset = sem("reset")

                def in_turn(eng, stages):
                    st.run(eng, BATCHES, [(0, stage) for _, stage in stages])

                with nc.Block() as block:
                    @block.sync
                    def _(_):
                        weights()
                        in_turn(sp, nodes["sp"])
                        ended()

                    @block.scalar
                    def _(_):
                        in_turn(act, nodes["act"])

                    @block.tensor
                    def _(_):
                        weights_ready()
                        in_turn(pe, nodes["pe"])

                    @block.vector
                    def _(_):
                        windows_reset(reset)
                        in_turn(dve, nodes["dve"])

                sem.join()

        passes = nc.values_load(choice[0:1, 0:1], min_val=1, max_val=N // WINDOW + 1)
        regular = nc.values_load(choice[0:1, 1:2], min_val=0, max_val=1)
        with nc.If(regular == 1):
            together(0)
            together(1)
        with nc.Else():
            apart(0)
            apart(1)


_INS = ["x", "src", "dst", "edge_attr_128", "L0_gnn_W_msg", "L0_gnn_b_msg", "L0_gnn_W_upd", "L0_gnn_b_upd",
        "L0_gnn_gamma", "L0_gnn_beta", "L1_gnn_ln1_g", "L1_gnn_ln1_b", "L1_gnn_W_conv", "L1_gnn_b_conv",
        "L1_gnn_ln2_g", "L1_gnn_ln2_b", "L1_gnn_W1", "L1_gnn_b1", "L1_gnn_W2", "L1_gnn_b2"]


def kernel(**inputs):
    import numpy as np
    import concourse.bacc as bacc
    from concourse.bass_utils import run_bass_kernel_spmd as run

    nc = bacc.Bacc("TRN2", target_bir_lowering=False, num_devices=1)
    arrays, args = {}, []
    for name in _INS:
        a = np.ascontiguousarray(inputs[name])
        arrays[f"in_{name}"] = a
        args.append(nc.dram_tensor(f"in_{name}", a.shape, mybir.dt.from_np(a.dtype), kind="ExternalInput").ap())
    args.append(nc.dram_tensor("out_0", (N, D), F32, kind="ExternalOutput").ap())
    build(nc, *args)
    return run(nc, [arrays], core_ids=[0]).results[0]["out_0"]
```
